# Optimizing a Trainium2 kernel written in Bass

```python
import numpy as np
import jax
import jax.numpy as jnp

def _softmax(x, axis=-1):
    return jax.nn.softmax(x, axis=axis)

def _gelu(x):
    return jax.nn.gelu(x, approximate=True)

def _silu(x):
    return jax.nn.silu(x)

def _sigmoid(x):
    return jax.nn.sigmoid(x)

def _layernorm(x, axis=-1, eps=1e-05):
    m = jnp.mean(x, axis=axis, keepdims=True)
    v = jnp.var(x, axis=axis, keepdims=True)
    return (x - m) / jnp.sqrt(v + eps)

def _scatter_add(tgt, idx, src, axis=0):
    return tgt.at[idx].add(src)

def _segment_sum(src, seg, n):
    return jax.ops.segment_sum(src, seg, n)
kernel_name = 'mk_macaron_d2_jaxref_r8_3435a4'

def setup_inputs(seed: int=0):
    np.random.seed(seed)
    _w = jnp.asarray

    def _L0_attn_setup():
        import jax, jax.numpy as jnp
        import numpy as np
        D_MODEL, N_HEADS, N_KV, HEAD_DIM, D_LAT = (128, 8, 2, 128, 32)
        N_REP = N_HEADS // N_KV
        B, T = (2, 256)
        key = jax.random.key(seed)
        ks = jax.random.split(key, 8)
        s = lambda fan_in: 1.0 / np.sqrt(fan_in)
        return {'x': jax.random.normal(ks[0], (B, T, D_MODEL), jnp.float32), 'wq': jax.random.normal(ks[1], (D_MODEL, N_HEADS * HEAD_DIM), jnp.float32) * s(D_MODEL), 'wk_down': jax.random.normal(ks[2], (D_MODEL, N_KV * D_LAT), jnp.float32) * s(D_MODEL), 'wv_down': jax.random.normal(ks[3], (D_MODEL, N_KV * D_LAT), jnp.float32) * s(D_MODEL), 'wk_up': jax.random.normal(ks[4], (D_LAT, HEAD_DIM), jnp.float32) * s(D_LAT), 'wv_up': jax.random.normal(ks[5], (D_LAT, HEAD_DIM), jnp.float32) * s(D_LAT), 'wo': jax.random.normal(ks[6], (N_HEADS * HEAD_DIM, D_MODEL), jnp.float32) * s(N_HEADS * HEAD_DIM)}
    _L0_attn_in = _L0_attn_setup()

    def _L0_ffn_setup():
        import jax, jax.numpy as jnp
        import numpy as np
        B, T, D, E = (4, 128, 128, 8)
        HD = 4 * D
        key = jax.random.key(seed)
        k1, k2, k3, k4 = jax.random.split(key, 4)
        std = 0.5 * D ** (-0.5)
        bound = 3.0 ** 0.5 * std
        x = jax.random.normal(k1, (B, T, D), dtype=jnp.float32)
        router_w = jax.random.normal(k2, (E, D), dtype=jnp.float32) * 0.02
        expert_fc = jax.random.uniform(k3, (E, D, HD), dtype=jnp.float32, minval=-bound, maxval=bound)
        expert_proj = jax.random.normal(k4, (E, D, HD), dtype=jnp.float32) * 0.02
        return {'x': x, 'router_w': router_w, 'expert_fc': expert_fc, 'expert_proj': expert_proj}
    _L0_ffn_in = _L0_ffn_setup()

    def _L1_attn_setup():
        import jax, jax.numpy as jnp
        import numpy as np
        H = 16
        G = 4
        THETA = 10000.0

        def _rope(x, cos, sin):
            x0 = x[..., ::2]
            x1 = x[..., 1::2]
            r0 = x0 * cos - x1 * sin
            r1 = x0 * sin + x1 * cos
            return jnp.stack([r0, r1], axis=-1).reshape(x.shape)
        key = jax.random.key(seed)
        ks = jax.random.split(key, 5)
        B, S, D = (2, 256, 128)
        return {'x': jax.random.normal(ks[0], (B, S, D), jnp.float32), 'Wq': jax.random.normal(ks[1], (D, D), jnp.float32) * 0.02, 'Wk': jax.random.normal(ks[2], (D, D // G), jnp.float32) * 0.02, 'Wv': jax.random.normal(ks[3], (D, D // G), jnp.float32) * 0.02, 'Wo': jax.random.normal(ks[4], (D, D), jnp.float32) * 0.02}
    _L1_attn_in = _L1_attn_setup()

    def _L1_ffn_setup():
        import jax, jax.numpy as jnp
        import numpy as np
        TOPK = 4
        key = jax.random.key(seed)
        ks = jax.random.split(key, 9)
        B, T, D = (4, 256, 128)
        E, H = (32, 128)
        HS = H * TOPK
        s = lambda k, shape, fan: jax.random.normal(k, shape, dtype=jnp.float32) / np.sqrt(fan)
        return {'x': jax.random.normal(ks[0], (B, T, D), dtype=jnp.float32), 'router_w': s(ks[1], (E, D), D), 'router_bias': jnp.zeros((E,), dtype=jnp.float32), 'gate_w': s(ks[2], (E, H, D), D), 'up_w': s(ks[3], (E, H, D), D), 'down_w': s(ks[4], (E, D, H), H), 'sgate_w': s(ks[5], (HS, D), D), 'sup_w': s(ks[6], (HS, D), D), 'sdown_w': s(ks[7], (D, HS), HS)}
    _L1_ffn_in = _L1_ffn_setup()
    _d = {'L0_attn_x': _L0_attn_in['x'], 'L0_attn_wq': _L0_attn_in['wq'], 'L0_attn_wk_down': _L0_attn_in['wk_down'], 'L0_attn_wv_down': _L0_attn_in['wv_down'], 'L0_attn_wk_up': _L0_attn_in['wk_up'], 'L0_attn_wv_up': _L0_attn_in['wv_up'], 'L0_attn_wo': _L0_attn_in['wo'], 'L0_ffn_router_w': _L0_ffn_in['router_w'], 'L0_ffn_expert_fc': _L0_ffn_in['expert_fc'], 'L0_ffn_expert_proj': _L0_ffn_in['expert_proj'], 'L1_attn_Wq': _L1_attn_in['Wq'], 'L1_attn_Wk': _L1_attn_in['Wk'], 'L1_attn_Wv': _L1_attn_in['Wv'], 'L1_attn_Wo': _L1_attn_in['Wo'], 'L1_ffn_router_w': _L1_ffn_in['router_w'], 'L1_ffn_router_bias': _L1_ffn_in['router_bias'], 'L1_ffn_gate_w': _L1_ffn_in['gate_w'], 'L1_ffn_up_w': _L1_ffn_in['up_w'], 'L1_ffn_down_w': _L1_ffn_in['down_w'], 'L1_ffn_sgate_w': _L1_ffn_in['sgate_w'], 'L1_ffn_sup_w': _L1_ffn_in['sup_w'], 'L1_ffn_sdown_w': _L1_ffn_in['sdown_w']}
    _x0 = _d['L0_attn_x']
    _d['L0_attn_x'] = jax.random.normal(jax.random.fold_in(jax.random.key(seed), 1), (16, 256, 128), dtype=_x0.dtype)
    del _x0
    return _d

def reference(L0_attn_x, L0_attn_wq, L0_attn_wk_down, L0_attn_wv_down, L0_attn_wk_up, L0_attn_wv_up, L0_attn_wo, L0_ffn_router_w, L0_ffn_expert_fc, L0_ffn_expert_proj, L1_attn_Wq, L1_attn_Wk, L1_attn_Wv, L1_attn_Wo, L1_ffn_router_w, L1_ffn_router_bias, L1_ffn_gate_w, L1_ffn_up_w, L1_ffn_down_w, L1_ffn_sgate_w, L1_ffn_sup_w, L1_ffn_sdown_w):

    def _L0_attn_ref(x, wq, wk_down, wv_down, wk_up, wv_up, wo):
        import jax, jax.numpy as jnp
        import numpy as np
        D_MODEL, N_HEADS, N_KV, HEAD_DIM, D_LAT = (128, 8, 2, 128, 32)
        N_REP = N_HEADS // N_KV
        B, T = (2, 256)
        Bq, Tq, _ = x.shape
        scale = HEAD_DIM ** (-0.5)
        q = (x @ wq).reshape(Bq, Tq, N_KV, N_REP, HEAD_DIM)
        k_lat = (x @ wk_down).reshape(Bq, Tq, N_KV, D_LAT)
        v_lat = (x @ wv_down).reshape(Bq, Tq, N_KV, D_LAT)
        k = jnp.einsum('bkhl,ld->bkhd', k_lat, wk_up)
        v = jnp.einsum('bkhl,ld->bkhd', v_lat, wv_up)
        scores = jnp.einsum('bqhrd,bkhd->bhrqk', q, k) * scale
        causal = jnp.tril(jnp.ones((Tq, Tq), dtype=bool))
        scores = jnp.where(causal, scores, jnp.finfo(scores.dtype).min)
        probs = jax.nn.softmax(scores, axis=-1)
        y = jnp.einsum('bhrqk,bkhd->bqhrd', probs, v)
        y = y.reshape(Bq, Tq, N_HEADS * HEAD_DIM)
        return y @ wo

    def _L0_ffn_ref(x, router_w, expert_fc, expert_proj):
        import jax, jax.numpy as jnp
        import numpy as np
        B, T, D, E = (4, 128, 128, 8)
        HD = 4 * D
        logits = jnp.einsum('btd,ed->bte', x, router_w)
        probs = jax.nn.softmax(logits, axis=-1)
        expert_ids = jnp.argmax(probs, axis=-1)
        mask = jax.nn.one_hot(expert_ids, E, dtype=x.dtype)
        h = jnp.einsum('btd,edh->ebth', x, expert_fc)
        h = jnp.square(jax.nn.relu(h))
        out_e = jnp.einsum('ebth,edh->ebtd', h, expert_proj)
        output = jnp.einsum('ebtd,bte->btd', out_e, mask)
        return output

    def _L1_attn_ref(x, Wq, Wk, Wv, Wo):
        import jax, jax.numpy as jnp
        import numpy as np
        H = 16
        G = 4
        THETA = 10000.0

        def _rope(x, cos, sin):
            x0 = x[..., ::2]
            x1 = x[..., 1::2]
            r0 = x0 * cos - x1 * sin
            r1 = x0 * sin + x1 * cos
            return jnp.stack([r0, r1], axis=-1).reshape(x.shape)
        B, S, D = x.shape
        hd = D // H
        Hkv = H // G
        q = x @ Wq
        k = x @ Wk
        v = x @ Wv
        k = jnp.repeat(k.reshape(B, S, Hkv, hd), G, axis=2)
        v = jnp.repeat(v.reshape(B, S, Hkv, hd), G, axis=2)
        inv = 1.0 / THETA ** (jnp.arange(0, D, 2, dtype=jnp.float32) / D)
        ang = jnp.arange(S, dtype=jnp.float32)[:, None] * inv[None, :]
        q = _rope(q, jnp.cos(ang)[None], jnp.sin(ang)[None])
        angk = ang[:, :hd // 2]
        k = _rope(k, jnp.cos(angk)[None, :, None, :], jnp.sin(angk)[None, :, None, :])
        q = q.reshape(B, S, H, hd).transpose(0, 2, 1, 3)
        k = k.transpose(0, 2, 1, 3)
        v = v.transpose(0, 2, 1, 3)
        scores = jnp.einsum('bhqd,bhkd->bhqk', q, k) / jnp.sqrt(jnp.float32(D))
        p = jax.nn.softmax(scores, axis=-1)
        o = jnp.einsum('bhqk,bhkd->bhqd', p, v)
        o = o.transpose(0, 2, 1, 3).reshape(B, S, D)
        return o @ Wo

    def _L1_ffn_ref(x, router_w, router_bias, gate_w, up_w, down_w, sgate_w, sup_w, sdown_w):
        import jax, jax.numpy as jnp
        import numpy as np
        TOPK = 4
        B, T, D = x.shape
        flat = x.reshape(B * T, D)
        logits = flat.astype(jnp.float32) @ router_w.T + router_bias
        scores = jax.nn.softmax(logits, axis=-1)
        topk_scores, topk_idx = jax.lax.top_k(scores, TOPK)
        topk_scores = topk_scores / jnp.clip(topk_scores.sum(axis=-1, keepdims=True), 1e-12, None)
        h = jax.nn.silu(jnp.einsum('nd,ehd->neh', flat, gate_w)) * jnp.einsum('nd,ehd->neh', flat, up_w)
        expert_out = jnp.einsum('neh,edh->ned', h, down_w)
        sel = jnp.take_along_axis(expert_out, topk_idx[:, :, None], axis=1)
        out = (sel * topk_scores.astype(flat.dtype)[:, :, None]).sum(axis=1)
        out = out + jax.nn.silu(flat @ sgate_w.T) * (flat @ sup_w.T) @ sdown_w.T
        return out.reshape(B, T, D)
    x = L0_attn_x
    x = x + 0.5 * _L0_ffn_ref(_layernorm(x, axis=-1), L0_ffn_router_w, L0_ffn_expert_fc, L0_ffn_expert_proj)
    x = x + _L0_attn_ref(_layernorm(x, axis=-1), L0_attn_wq, L0_attn_wk_down, L0_attn_wv_down, L0_attn_wk_up, L0_attn_wv_up, L0_attn_wo)
    x = x + 0.5 * _L0_ffn_ref(_layernorm(x, axis=-1), L0_ffn_router_w, L0_ffn_expert_fc, L0_ffn_expert_proj)
    x = x + 0.5 * _L1_ffn_ref(_layernorm(x, axis=-1), L1_ffn_router_w, L1_ffn_router_bias, L1_ffn_gate_w, L1_ffn_up_w, L1_ffn_down_w, L1_ffn_sgate_w, L1_ffn_sup_w, L1_ffn_sdown_w)
    x = x + _L1_attn_ref(_layernorm(x, axis=-1), L1_attn_Wq, L1_attn_Wk, L1_attn_Wv, L1_attn_Wo)
    x = x + 0.5 * _L1_ffn_ref(_layernorm(x, axis=-1), L1_ffn_router_w, L1_ffn_router_bias, L1_ffn_gate_w, L1_ffn_up_w, L1_ffn_down_w, L1_ffn_sgate_w, L1_ffn_sup_w, L1_ffn_sdown_w)
    return x

_drawn_inputs = setup_inputs


def setup_inputs(seed=0):
    import zlib

    import numpy as np

    out = dict(_drawn_inputs(seed))
    spreads = {'L1_ffn_router_bias': (0.0, 0.1)}
    factors = {'L1_attn_Wq': 8.0, 'L1_attn_Wk': 8.0, 'L1_attn_Wv': 7.826, 'L1_attn_Wo': 6.846}
    for name, (base, spread) in spreads.items():
        noise = np.random.default_rng([zlib.crc32(name.encode()), seed]).standard_normal(out[name].shape)
        drawn = base * np.exp(spread * noise) if base else spread * noise
        out[name] = jnp.asarray(drawn.astype(out[name].dtype))
    for name, factor in factors.items():
        out[name] = (out[name] * factor).astype(out[name].dtype)
    return out
```

```python
import numpy as np
import concourse.bass as bass
from concourse import mybir
from contextlib import ExitStack

F32, F16, BF16, I32, U32 = (mybir.dt.float32, mybir.dt.float16, mybir.dt.bfloat16, mybir.dt.int32,
                            mybir.dt.uint32)
ALU = mybir.AluOpType
ACT = mybir.ActivationFunctionType
AX = mybir.AxisListType

P = 128
D = 128
TOKENS = 4096
NT = TOKENS // P
GT = 4
NG = NT // GT
GC = GT * P
EPS = 1e-5

SX, SW, SP = 2.0 ** 8, 2.0 ** 8, 2.0 ** 10
LOGSP = 10 * float(np.log(2.0))
ROUND = 2.0 ** 23


class Moe:

    def __init__(self, tag, E, K, J, H, SH):
        self.tag, self.E, self.K, self.J, self.H, self.SH = tag, E, K, J, H, SH
        self.ET = E * NT
        self.HC = H // P
        blocks = TOKENS * K // P + E - 1
        self.steps = -(-blocks // J)
        self.steps += -self.steps % 4
        self.blocks = self.steps * J
        self.YC = 0.5 / (SH * SW)


L0 = Moe("top1", E=8, K=1, J=2, H=512, SH=2.0 ** 4)
L1 = Moe("top4", E=32, K=4, J=4, H=128, SH=2.0 ** 6)
AREA_WORDS = 15040
SC = 4
HEADS, KV, LAT = 8, 2, 32
BATCH = 16
PHASES = ["moe0", "attn0", "moe0", "moe1", "attn1", "moe1"]


class Signal:
    def __init__(self, sem):
        self.sem, self.base = sem, 0

    def at(self, n):
        return self.sem, n + self.base


def stepped(eng, steps, body, unroll=4):
    for s in range(unroll):
        body(s, s)
    with eng.Fori(1, steps // unroll - 1) as i:
        for u in range(unroll):
            body(i * unroll + u, u)
    for u in range(unroll):
        body(steps - unroll + u, u)


def first_peeled(eng, turns, body):
    body(0)
    with eng.Fori(1, turns) as i:
        body(i)


def is_static(s):
    return isinstance(s, int)


def wait(eng, signal, n):
    if not is_static(n) or n > 0:
        eng.wait_ge(*signal.at(n))


def build(nc, a, out, phases=None):
    phases = phases or PHASES
    ctx = ExitStack()
    with ctx:
        def sb(name, shape, dt):
            return ctx.enter_context(nc.sbuf_tensor(name, shape, dt))

        def signal(name):
            return Signal(ctx.enter_context(nc.semaphore(name)))

        X = sb("X", [P, NT * D], F32)
        XH = sb("XH", [P, NT * 2 * D], F16)
        XT = sb("XT", [P, NG * 2 * GC], F16)
        XH4 = XH[:, :].rearrange("p (t h d) -> p t h d", h=2, d=D)
        FC = [sb(f"FC{i}", [P, L0.E * 512], F16) for i in range(2)]
        PJ = [sb(f"PJ{i}", [P, L0.E * 512], F16) for i in range(2)]
        WG = [sb(f"WG{i}", [P, L1.E * P], F16) for i in range(2)]
        WU = [sb(f"WU{i}", [P, L1.E * P], F16) for i in range(2)]
        WD = [sb(f"WD{i}", [P, L1.E * P], F16) for i in range(2)]
        SG = [sb(f"SG{i}", [P, SC * P], F16) for i in range(2)]
        SU = [sb(f"SU{i}", [P, SC * P], F16) for i in range(2)]
        SD = [sb(f"SD{i}", [P, SC * D], F16) for i in range(2)]
        RW = {L.tag: [sb(f"RW{L.tag}{i}", [P, L.E], F16) for i in range(2)] for L in (L0, L1)}
        BIAS = sb("BIAS", [P, L1.E], F32)
        IDH = sb("IDH", [P, P], F16)
        IDF = sb("IDF", [P, P], F32)
        TRI = sb("TRI", [P, P], F16)
        ONES = sb("ONES", [P, P], F16)
        IOTAE = sb("IOTAE", [P, L1.E], F32)
        IOTAB = sb("IOTAB", [P, 2], F32)
        STAT = sb("STAT", [P, NT, 6], F32)
        MEAN, VAR, TMPS, RSTD, ZSUM = (sb(n, [P, NT], F32) for n in ("MEAN", "VAR", "TMPS", "RSTD", "ZSUM"))
        HALFNEG = sb("HALFNEG", [P, NT], F32)
        M8 = sb("M8", [P, NT, 8], F32)
        I8 = sb("I8", [P, NT, 8], U32)
        IF = sb("IF", [P, NT, 8], F32)
        CNT = sb("CNT", [P, L1.E + 1], F32)
        NBE, BEND, ADJ, CMP = (sb(n, [P, L1.E], F32) for n in ("NBE", "BEND", "ADJ", "CMP"))
        SPARE = sb("SPARE", [P, 1], F32)
        BEX = sb("BEX", [P, 2], F32)
        BTAB = sb("BTAB", [1, 2 * P], I32)
        DST = sb("DST", [P, NT * 4], F32)
        DSI = [sb(f"DSI{i}", [P, NT * 4], I32) for i in range(3)]
        ROW = sb("ROW", [P, NT * 4], I32)
        W4 = sb("W4", [P, NT, 4], F32)
        ZERO = sb("ZERO", [P, GT * 2 * D], F16)

        AREA = sb("AREA", [P, AREA_WORDS], F32)
        area_at = [0]

        def area(shape, dt, start=None):
            if start is not None:
                area_at[0] = start
            n = int(np.prod(shape))
            words = n if dt == F32 else -(-n // 2)
            v = AREA[:, area_at[0]:area_at[0] + words]
            area_at[0] += words
            assert area_at[0] <= AREA_WORDS
            v = v if dt == F32 else v.bitcast(dt)
            if len(shape) == 2:
                v = v.rearrange("p (a b) -> p a b", b=shape[1])
            if len(shape) == 3:
                v = v.rearrange("p (a b c) -> p a b c", b=shape[1], c=shape[2])
            return v

        LNT = area([NT * D], F32, 0)
        LG = area([L1.ET], F32, 0)
        EX = area([L1.ET], F32)
        OH = [area([L1.ET], F16) for _ in range(4)]
        MH = area([L1.ET], F16)
        CUM = area([L1.ET], F32)
        SLOT = area([L1.ET], F32)
        PICK = area([L1.ET], F32)
        XG = area([4, 4 * 2 * D], F16, 0)
        XTB = area([2, 4 * 2 * P], F16)
        HA = area([1024], F32)
        HF = area([2, 1024], F32)
        HH = [area([2, 2048], F16) for _ in range(2)]
        YS = area([2, 4 * D], F32)
        YG = area([2, GT * 4 * D], F32, 0)
        AH = [area([HEADS * D], F16, 0), area([HEADS * D], F16)]
        BH = [area([HEADS * D], F16) for _ in range(2)]
        ZB = [area([2, 512], F16) for _ in range(2)]
        PF = area([2, 768], F32)
        PTB = [area([2, 768], F16) for _ in range(2)]
        OB = [area([2, 512], F16) for _ in range(2)]
        NM = area([2, 4], F32)
        RS = area([2, 4], F32)
        MASK = area([P], BF16)
        IDB = area([P], BF16)
        MASKF = area([P], F32)
        WQT = area([HEADS * D], F32)
        WOH = area([HEADS * D], F32)
        WLAT = [area([KV * D], F32) for _ in range(2)]
        WUPS = [area([P], F32) for _ in range(2)]
        WKV = [area([KV * D], F32) for _ in range(2)]
        AW = [area([352], F16, 0), area([352], F16)]
        AO = [area([D], F16) for _ in range(2)]
        COS, SIN = (area([2, 160], F32) for _ in range(2))
        MASKR = area([4], F32)
        LNSP = area([1], F32)
        RT = area([2, 160], F32)
        RF = area([2, 160], F32)
        QP = [area([16, 32], F16) for _ in range(4)]
        KP = area([4, 4, 32], F16)
        KTB = area([2, 512], F16)
        VP = area([NT, 68], F16)
        QT1, QT2 = (area([2, 512], F16) for _ in range(2))
        MX = area([2, 16], F32)
        PF1 = area([4, 1024], F32)
        PB1 = [area([4, 1024], F16) for _ in range(2)]
        OS = area([16 * 17], F32)
        ON = area([16, 8], F32)
        RC = area([16], F32)
        ONB = [area([P], F16) for _ in range(2)]
        OTB = area([2 * P], F16)
        WST = PF1[:, 0, 0:352 + P]
        STG = area([3, 2048], F32, 7680)

        PS = ctx.enter_context(nc.psum_tensor("PS", [P, 8, 512], F32))

        def banks(b, n=1):
            return PS[:, b:b + n, :].rearrange("p b c -> p (b c)")

        for L in (L0, L1):
            L.xs = nc.dram_tensor(f"slots_{L.tag}", [L.blocks * P, 2 * D], F16, kind="Internal").ap()
            L.ys = nc.dram_tensor(f"results_{L.tag}", [L.blocks * P, D], F32, kind="Internal").ap()

        x_loaded, bias_loaded = signal("x_loaded"), signal("bias_loaded")
        staged = [signal(f"weights_staged{u}") for u in range(3)]
        w_hi, w_lo = signal("weights_hi"), signal("weights_lo")
        zeros, filled = signal("zeros_ready"), {L.tag: signal("slots_zeroed_" + L.tag) for L in (L0, L1)}
        cst_step, consts = signal("constant_steps"), signal("constants_ready")
        written = signal("output_written")
        ln_stat, ln_step, ln_var, ln_rstd = (signal("ln_" + n) for n in ("statistics", "steps", "var", "rstd"))
        ln_norm, ln_hi, ln_lo = signal("ln_normed"), signal("ln_hi"), signal("ln_lo")
        ln_tr = signal("ln_transposed")
        ln_xt = [signal(f"ln_xt_ready{u}") for u in range(2)]
        logits, rt_step, rt_shift, rt_exp = (signal("logits"), signal("route_steps"), signal("route_shifted"),
                                             signal("route_exp"))
        rt_choice, rt_pos, rt_bex, rt_brow, rt_tab, rt_row = (signal(n) for n in (
            "choices", "positions", "block_experts", "block_expert_row", "block_table", "rows"))
        dp_sent = signal("dispatched")
        sh_gu, sh_silu, sh_h, sh_hi, sh_lo, sh_y, sh_add = (signal(n) for n in (
            "shared_up", "shared_silu", "shared_hidden", "shared_hi", "shared_lo", "shared_down", "shared_added"))
        bl_load = [signal(f"block_loaded{u}") for u in range(4)]
        bl_tr, bl_xt, bl_up, bl_act, bl_h, bl_hi, bl_lo, bl_dn, bl_y, bl_st = (signal(n) for n in (
            "block_transposed", "block_xt", "block_up", "block_act", "block_hidden", "block_hi", "block_lo",
            "block_down", "block_y", "block_stored"))
        cb_got, cb_add = ([signal(f"combine_gathered{u}") for u in range(2)],
                                    [signal(f"combine_added{u}") for u in range(2)])
        cb_step = signal("combine_steps")

        splits = []
        for name, (hi, lo), n in (("rw0", RW["top1"], L0.E), ("fc", FC, 4096), ("pj", PJ, 4096),
                                  ("wg", WG, 4096), ("wu", WU, 4096), ("wd", WD, 4096),
                                  ("sg", SG, 512), ("su", SU, 512), ("sd", SD, 512), ("rw1", RW["top4"], L1.E)):
            for c in range(0, n, 2048):
                m = min(2048, n - c)
                splits.append((a[name][:, c:c + m], hi[:, c:c + m], lo[:, c:c + m], m))
        FIRST = 1
        CONSTS = 5

        def product3(psum, lhs, rhs, start=True, stop=True, **kw):
            nc.tensor.matmul(psum, lhs[0], rhs[0], start=start, stop=False, **kw)
            nc.tensor.matmul(psum, lhs[0], rhs[1], start=False, stop=False, **kw)
            return nc.tensor.matmul(psum, lhs[1], rhs[0], start=False, stop=stop, **kw)

        def setup_sync(sp):
            sp.dma_start(X[:, :].rearrange("p (t d) -> p t d", d=D),
                         a["x"].rearrange("(t p) d -> p t d", p=P)).then_inc(x_loaded.sem, 16)
            sp.dma_start(BIAS[:, :], a["bias"]).then_inc(bias_loaded.sem, 16)
            for n, (src, hi, lo, m) in enumerate(splits):
                if n >= 3:
                    sp.wait_ge(*w_lo.at(n - 2))
                sp.dma_start(STG[:, n % 3, :m], src).then_inc(staged[n % 3].sem, 16)
                if n == 2:
                    sp.wait_ge(*zeros.at(1))
                    zero_slots(sp, L0)
            sp.wait_ge(*w_lo.at(len(splits)))

        def zero_slots(sp, L):
            sp.dma_start(L.xs.rearrange("(n p j) c -> p n (j c)", p=P, j=4),
                         ZERO[:, :].unsqueeze(1).to_broadcast([P, L.blocks // 4, GT * 2 * D])
                         ).then_inc(filled[L.tag].sem, 16)

        def setup_pool(pool):
            nc.gpsimd.memset(IDF[:, :], 0.0).then_inc(cst_step.sem, 1)
            nc.gpsimd.memset(ONES[:, :], 1.0).then_inc(cst_step.sem, 1)
            nc.gpsimd.memset(HALFNEG[:, :], -0.5).then_inc(consts.sem, 1)
            nc.gpsimd.iota(IOTAE[:, :], pattern=[[1, L1.E]], base=0, channel_multiplier=0,
                           allow_small_or_imprecise_dtypes=True).then_inc(consts.sem, 1)
            nc.gpsimd.iota(IOTAB[:, :], pattern=[[P, 2]], base=0, channel_multiplier=1,
                           allow_small_or_imprecise_dtypes=True).then_inc(consts.sem, 1)
            pool.wait_ge(*cst_step.at(2))
            nc.gpsimd.affine_select(out=IDF[:, :], in_=IDF[:, :], compare_op=ALU.not_equal, fill=1.0, base=0,
                                    pattern=[[-1, P]], channel_multiplier=1).then_inc(cst_step.sem, 1)
            nc.gpsimd.affine_select(out=TRI[:, :], in_=ONES[:, :], compare_op=ALU.is_gt, fill=0.0, base=0,
                                    pattern=[[1, P]], channel_multiplier=-1).then_inc(consts.sem, 1)
            pool.wait_ge(*cst_step.at(3))
            nc.gpsimd.tensor_copy(IDH[:, :], IDF[:, :]).then_inc(consts.sem, 1)

        def split_scalar(act, first, last):
            for n, (src, hi, lo, m) in list(enumerate(splits))[first:last]:
                act.wait_ge(*staged[n % 3].at(16 * (n // 3 + 1)))
                nc.scalar.activation(hi, STG[:, n % 3, :m], ACT.Copy, scale=SW).then_inc(w_hi.sem, 1)

        def split_vector(dve, first, last):
            for n, (src, hi, lo, m) in list(enumerate(splits))[first:last]:
                dve.wait_ge(*w_hi.at(n + 1))
                nc.vector.scalar_tensor_tensor(out=lo, in0=STG[:, n % 3, :m], scalar=SW, in1=hi,
                                               op0=ALU.mult, op1=ALU.subtract).then_inc(w_lo.sem, 1)

        class Chain:

            def __init__(self, eng, sig, n=0):
                self.eng, self.sig, self.n = eng, sig, n

            def __call__(self, ins):
                self.n += 1
                ins.then_inc(self.sig.sem, 1)
                self.eng.wait_ge(*self.sig.at(self.n))

        def statistics(tile):
            return nc.vector.bn_stats(STAT[:, bass.ds(tile, 1), :].rearrange("p a b -> p (a b)"),
                                      X[:, bass.ds(tile * D, D)]).then_inc(ln_stat.sem, 1)

        def ln_vector(dve, first):
            if first:
                with dve.Fori(0, NG) as g:
                    for j in range(GT):
                        statistics(g * GT + j)
            dve.wait_ge(*consts.at(CONSTS))
            dve.wait_ge(*ln_stat.at(NT))
            link = Chain(dve, ln_step)
            link(nc.vector.tensor_tensor(TMPS[:, :], STAT[:, :, 1], STAT[:, :, 4], ALU.subtract))
            link(nc.vector.tensor_tensor(VAR[:, :], STAT[:, :, 2], STAT[:, :, 5], ALU.add))
            link(nc.vector.tensor_scalar(VAR[:, :], VAR[:, :], 1.0 / (D * SX * SX), EPS / (SX * SX), ALU.mult,
                                         ALU.add))
            link(nc.vector.scalar_tensor_tensor(out=TMPS[:, :], in0=TMPS[:, :], scalar=0.25 / (SX * SX),
                                                in1=TMPS[:, :], op0=ALU.mult, op1=ALU.mult))
            nc.vector.tensor_tensor(VAR[:, :], VAR[:, :], TMPS[:, :], ALU.add).then_inc(ln_var.sem, 1)
            link(nc.vector.tensor_tensor(MEAN[:, :], STAT[:, :, 1], STAT[:, :, 4], ALU.add))
            link(nc.vector.tensor_scalar(MEAN[:, :], MEAN[:, :], 0.5, None, ALU.mult))

            def turn(i):
                for u in range(2):
                    g = i * 2 + u
                    for j in range(GT):
                        t = g * GT + j
                        ins = nc.vector.tensor_scalar(LNT[:, bass.ds(t * D, D)], X[:, bass.ds(t * D, D)],
                                                      MEAN[:, bass.ds(t, 1)], RSTD[:, bass.ds(t, 1)],
                                                      ALU.subtract, ALU.mult)
                    ins.then_inc(ln_norm.sem, 1)
                for u in range(2):
                    g = i * 2 + u
                    dve.wait_ge(*ln_hi.at(g + 1))
                    nc.vector.tensor_tensor(XH4[:, bass.ds(g * GT, GT), 1, :],
                                            LNT[:, bass.ds(g * GC, GC)].rearrange("p (t d) -> p t d", d=D),
                                            XH4[:, bass.ds(g * GT, GT), 0, :], ALU.subtract).then_inc(ln_lo.sem, 1)
            for half in range(2):
                dve.wait_ge(*ln_rstd.at(half + 1))
                with dve.Fori(half * NG // 4, (half + 1) * NG // 4) as i:
                    turn(i)

        def ln_pool(pool):
            pool.wait_ge(*ln_var.at(1))
            for half in range(2):
                c = slice(half * NT // 2, (half + 1) * NT // 2)
                nc.gpsimd.tensor_tensor(RSTD[:, c], VAR[:, c], HALFNEG[:, c], ALU.pow).then_inc(ln_rstd.sem, 1)

        def ln_scalar(act):
            def hi(i):
                for u in range(2):
                    g = i * 2 + u
                    act.wait_ge(*ln_norm.at(g + 1))
                    nc.scalar.activation(XH4[:, bass.ds(g * GT, GT), 0, :],
                                         LNT[:, bass.ds(g * GC, GC)].rearrange("p (t d) -> p t d", d=D),
                                         ACT.Copy).then_inc(ln_hi.sem, 1)

            def xt(i):
                for u in range(2):
                    act.wait_ge(*ln_tr.at(i * 2 + u + 1))
                    nc.scalar.activation(XT[:, bass.ds((i * 2 + u) * 2 * GC, 2 * GC)],
                                         banks(u).bitcast(F16), ACT.Copy).then_inc(ln_xt[u].sem, 1)
            hi(0)
            with act.Fori(1, NG // 2) as i:
                hi(i)
                xt(i - 1)
            xt(NG // 2 - 1)

        def ln_tensor(pe, L=None):
            pe.wait_ge(*consts.at(CONSTS))
            if L:
                pe.wait_ge(*w_lo.at(FIRST if L is L0 else len(splits)))

            def transposes(i, u):
                pe.wait_ge(*ln_lo.at(i * 2 + u + 1))
                wait(pe, ln_xt[u], i)
                bank = banks(u).bitcast(F16)
                for h in range(2):
                    for j in range(GT):
                        t = (i * 2 + u) * GT + j
                        ins = nc.tensor.transpose(bank[:, (h * GT + j) * P:(h * GT + j + 1) * P],
                                                  XH[:, bass.ds((t * 2 + h) * D, D)], IDH[:, :])
                ins.then_inc(ln_tr.sem, 1)

            def group_logits(i, u):
                g = i * 2 + u
                pe.wait_ge(*ln_xt[u].at(i + 1))
                for j in range(GT):
                    x = [XT[:, bass.ds(g * 2 * GC + h * GC + j * P, P)] for h in range(2)]
                    ins = product3(banks(2, 2)[:, bass.ds((g * GT + j) * L.E, L.E)], x,
                                   [w[:, :] for w in RW[L.tag]])
                ins.then_inc(logits.sem, 1)

            def turn(i):
                for u in range(2):
                    transposes(i, u)
                    if L and not (is_static(i) and i == 0):
                        group_logits(i - 1, u)
            first_peeled(pe, NG // 2, turn)
            if L:
                for u in range(2):
                    group_logits(NG // 2 - 1, u)

        LN_COUNTS = {ln_stat: NT, ln_step: 6, ln_var: 1, ln_rstd: 2, ln_norm: NG, ln_hi: NG, ln_lo: NG, ln_tr: NG,
                     ln_xt[0]: NG // 2, ln_xt[1]: NG // 2}

        def route_tensor(pe, L):
            pe.wait_ge(*rt_choice.at(1))
            for c in range(0, L.ET, 512):
                n = min(512, L.ET - c)
                nc.tensor.matmul(banks(4, 2)[:, c:c + n], TRI[:, :], MH[:, c:c + n], start=True, stop=True)
                ins = nc.tensor.matmul(banks(6, 2)[:, c:c + n], ONES[:, :], MH[:, c:c + n], start=True, stop=True)
            ins.then_inc(rt_pos.sem, 1)
            pe.wait_ge(*rt_bex.at(1))
            for c in range(2):
                ins = nc.tensor.transpose(banks(2)[0:1, c * P:(c + 1) * P], BEX[:, c:c + 1], IDF[:, :])
            ins.then_inc(rt_brow.sem, 1)

        def route_vector(dve, L):
            E, K, ET = L.E, L.K, L.ET
            link = Chain(dve, rt_step)
            lg = LG[:, :ET].rearrange("p (t e) -> p t e", e=E)
            ex = EX[:, :ET].rearrange("p (t e) -> p t e", e=E)

            def et(buf):
                return buf[:, :ET].rearrange("p (e t) -> p e t", t=NT)

            dve.wait_ge(*logits.at(NG))
            got = banks(2, 2)[:, :ET].rearrange("p (t e) -> p t e", e=E)
            if L is L1:
                dve.wait_ge(*bias_loaded.at(16))
                link(nc.vector.scalar_tensor_tensor(out=lg, in0=got, scalar=1.0 / (SX * SW),
                                                    in1=BIAS[:, :].unsqueeze(1).to_broadcast([P, NT, E]),
                                                    op0=ALU.mult, op1=ALU.add))
            else:
                link(nc.vector.tensor_scalar(lg, got, 1.0 / (SX * SW), None, ALU.mult))
            for t in range(NT):
                ins = nc.vector.max(M8[:, t, :], lg[:, t, :])
            link(ins)
            for t in range(NT):
                ins = nc.vector.max_index(I8[:, t, :], M8[:, t, :], lg[:, t, :])
            link(ins)
            link(nc.vector.tensor_copy(IF[:, :, :], I8[:, :, :]))
            if L is L1:
                nc.vector.tensor_tensor(ex, lg, M8[:, :, 0:1].to_broadcast([P, NT, E]),
                                        ALU.subtract).then_inc(rt_shift.sem, 1)
                nc.vector.tensor_tensor(W4[:, :, :], M8[:, :, 0:4], M8[:, :, 0:1].to_broadcast([P, NT, 4]),
                                        ALU.subtract).then_inc(rt_shift.sem, 1)
            for k in range(K):
                ins = nc.vector.tensor_tensor(et(OH[k]), IOTAE[:, :E].unsqueeze(2).to_broadcast([P, E, NT]),
                                              IF[:, :, k].unsqueeze(1).to_broadcast([P, E, NT]), ALU.is_equal)
            link(ins)
            if K == 1:
                nc.vector.tensor_copy(MH[:, :ET], OH[0][:, :ET]).then_inc(rt_choice.sem, 1)
            else:
                link(nc.vector.tensor_tensor(SLOT[:, :ET], OH[0][:, :ET], OH[1][:, :ET], ALU.add))
                link(nc.vector.tensor_tensor(PICK[:, :ET], OH[2][:, :ET], OH[3][:, :ET], ALU.add))
                nc.vector.tensor_tensor(MH[:, :ET], SLOT[:, :ET], PICK[:, :ET], ALU.add).then_inc(rt_choice.sem, 1)
            dve.wait_ge(*rt_pos.at(1))
            pos, tot = banks(4, 2)[:, :ET], banks(6, 2)[:, :ET]
            one = ONES[:, 0:1]
            link(nc.vector.tensor_tensor_scan(CUM[:, :ET], one.to_broadcast([P, ET]), tot, 0.0,
                                              ALU.mult, ALU.add))
            nc.vector.memset(CNT[:, 0:1], 0.0)
            link(nc.vector.tensor_copy(CNT[:, 1:E + 1], et(CUM)[:, :, NT - 1]))
            link(nc.vector.tensor_tensor(SLOT[:, :ET], CUM[:, :ET], tot, ALU.subtract))
            link(nc.vector.tensor_tensor(NBE[:, :E], CNT[:, 1:E + 1], CNT[:, 0:E], ALU.subtract))
            link(nc.vector.tensor_scalar(NBE[:, :E], NBE[:, :E], 1.0 / P, 0.5 - 0.5 / P, ALU.mult, ALU.add))
            link(nc.vector.tensor_scalar(NBE[:, :E], NBE[:, :E], ROUND, None, ALU.add))
            link(nc.vector.tensor_scalar(NBE[:, :E], NBE[:, :E], -ROUND, None, ALU.add))
            link(nc.vector.tensor_tensor_scan(BEND[:, :E], one.to_broadcast([P, E]), NBE[:, :E], 0.0,
                                              ALU.mult, ALU.add))
            link(nc.vector.tensor_tensor(ADJ[:, :E], BEND[:, :E], NBE[:, :E], ALU.subtract))
            link(nc.vector.scalar_tensor_tensor(out=ADJ[:, :E], in0=ADJ[:, :E], scalar=float(P), in1=CNT[:, 0:E],
                                                op0=ALU.mult, op1=ALU.subtract))
            for c in range(2):
                link(nc.vector.tensor_scalar(CMP[:, :E], BEND[:, :E], IOTAB[:, c:c + 1], None, ALU.is_le))
                link(nc.vector.reduce_sum(BEX[:, c:c + 1], CMP[:, :E], axis=AX.X))
            nc.vector.tensor_scalar(BEX[:, :], BEX[:, :], float(E - 1), None, ALU.min).then_inc(rt_bex.sem, 1)
            link(nc.vector.tensor_tensor(SLOT[:, :ET], SLOT[:, :ET], pos, ALU.add))
            link(nc.vector.tensor_tensor(et(SLOT), et(SLOT), ADJ[:, :E].unsqueeze(2).to_broadcast([P, E, NT]),
                                         ALU.add))
            for k in range(K):
                link(nc.vector.tensor_tensor(PICK[:, :ET], OH[k][:, :ET], SLOT[:, :ET], ALU.mult))
                link(nc.vector.reduce_sum(DST[:, k:NT * K:K], PICK[:, :ET].rearrange("p (e t) -> p t e", t=NT),
                                          axis=AX.X))
            lj, m = L.J.bit_length() - 1, NT * K
            link(nc.vector.tensor_copy(DSI[0][:, :m], DST[:, :m]))
            link(nc.vector.tensor_scalar(DSI[1][:, :m], DSI[0][:, :m], P - 1, lj, ALU.bitwise_and,
                                         ALU.logical_shift_left))
            link(nc.vector.tensor_scalar(DSI[2][:, :m], DSI[0][:, :m], 7, L.J - 1, ALU.arith_shift_right,
                                         ALU.bitwise_and))
            link(nc.vector.tensor_tensor(DSI[1][:, :m], DSI[1][:, :m], DSI[2][:, :m], ALU.bitwise_or))
            link(nc.vector.tensor_scalar(DSI[2][:, :m], DSI[0][:, :m], ~(L.J * P - 1), None, ALU.bitwise_and))
            nc.vector.tensor_tensor(ROW[:, :m], DSI[1][:, :m], DSI[2][:, :m], ALU.bitwise_or
                                    ).then_inc(rt_row.sem, 1)
            dve.wait_ge(*rt_brow.at(1))
            nc.vector.tensor_copy(BTAB[:, :], banks(2)[0:1, 0:2 * P]).then_inc(rt_tab.sem, 1)
            if L is L1:
                def per_tile(buf):
                    return buf[:, :].unsqueeze(2).to_broadcast([P, NT, 4])
                dve.wait_ge(*rt_exp.at(2))
                link(nc.vector.reduce_sum(ZSUM[:, :], ex, axis=AX.X))
                link(nc.vector.reciprocal(ZSUM[:, :], ZSUM[:, :]))
                link(nc.vector.tensor_tensor(W4[:, :, :], W4[:, :, :], per_tile(ZSUM), ALU.mult))
                link(nc.vector.reduce_sum(ZSUM[:, :], W4[:, :, :], axis=AX.X))
                link(nc.vector.tensor_scalar(ZSUM[:, :], ZSUM[:, :], 1e-12, None, ALU.max))
                link(nc.vector.reciprocal(ZSUM[:, :], ZSUM[:, :]))
                link(nc.vector.scalar_tensor_tensor(out=W4[:, :, :], in0=W4[:, :, :], scalar=L.YC,
                                                    in1=per_tile(ZSUM), op0=ALU.mult, op1=ALU.mult))

        def route_steps(L):
            return (1 + 2 + 1 + 1 + (0 if L.K == 1 else 2) + 1 + 1 + 1 + 4 + 1 + 2 + 4 + 2 + 2 * L.K + 5
                    + (7 if L is L1 else 0))

        def route_scalar(act, L):
            if L is L1:
                ex = EX[:, :L.ET]
                for n, v in enumerate((ex, W4[:, :, :])):
                    act.wait_ge(*rt_shift.at(n + 1))
                    nc.scalar.activation(v, v, ACT.Exp).then_inc(rt_exp.sem, 1)

        def carry_wait():
            nc.gpsimd.tensor_tensor(SPARE[0:1, :], HALFNEG[0:1, 0:1], HALFNEG[0:1, 0:1], ALU.add)

        def dispatch_pool(pool, L):
            pool.wait_ge(*rt_row.at(1))
            pool.wait_ge(*filled[L.tag].at(16))
            for n in range(NT * L.K):
                t = n // L.K
                nc.gpsimd.indirect_dma_start(
                    out=L.xs, out_offset=bass.IndirectOffsetOnAxis(ap=ROW[:, n:n + 1], axis=0),
                    in_=XH[:, t * 2 * D:(t + 1) * 2 * D], in_offset=None).then_inc(dp_sent.sem, 16)

        def shared_tensor(pe):
            pe.wait_ge(*w_lo.at(len(splits)))
            pe.wait_ge(*rt_tab.at(1))

            def up(g, v, j, first):
                n = g * SC + j
                if not first:
                    pe.wait_ge(*sh_h.at(n - 1))
                for b, w in ((j % 2, SG), (2 + j % 2, SU)):
                    ins = product3(banks(b), [w[h][:, j * P:(j + 1) * P] for h in range(2)],
                                   [XT[:, bass.ds(g * 2 * GC + h * GC, GC)] for h in range(2)])
                ins.then_inc(sh_gu.sem, 1)

            def down(g, v, first):
                pe.wait_ge(*sh_lo.at(g * SC + SC))
                if not first:
                    pe.wait_ge(*sh_add.at(g))
                for t in range(GT):
                    for j in range(SC):
                        ins = product3(banks(4)[:, t * D:(t + 1) * D],
                                       [HH[h][:, v, j * GC + t * P:j * GC + (t + 1) * P] for h in range(2)],
                                       [SD[h][:, j * D:(j + 1) * D] for h in range(2)], j == 0, j == SC - 1)
                ins.then_inc(sh_y.sem, 1)

            def group(g, v):
                for j in range(SC):
                    up(g, v, j, is_static(g) and g == 0 and j < 2)
                    if j == 1 and not (is_static(g) and g == 0):
                        down(g - 1, 1 - v, is_static(g) and g == 1)
            stepped(pe, NG, group, 2)
            down(NG - 1, 1, False)

        def shared_scalar(act):
            def group(g, v):
                for j in range(SC):
                    n = g * SC + j
                    act.wait_ge(*sh_gu.at(n + 1))
                    if not (is_static(g) and g == 0 and j < 2):
                        act.wait_ge(*sh_h.at(n - 1))
                    nc.scalar.activation(HA[:, (j % 2) * GC:(j % 2 + 1) * GC], banks(j % 2), ACT.Silu,
                                         scale=1.0 / (SX * SW)).then_inc(sh_silu.sem, 1)
                    act.wait_ge(*sh_h.at(n + 1))
                    if not (is_static(g) and g < 2):
                        act.wait_ge(*sh_y.at(g - 1))
                    nc.scalar.activation(HH[0][:, v, j * GC:(j + 1) * GC], HF[:, j % 2, :GC], ACT.Copy
                                         ).then_inc(sh_hi.sem, 1)
            stepped(act, NG, group, 2)

        def shared_vector(dve):
            def add(g):
                dve.wait_ge(*sh_y.at(g + 1))
                x = X[:, bass.ds(g * GC, GC)] if not is_static(g) else X[:, g * GC:(g + 1) * GC]
                nc.vector.scalar_tensor_tensor(out=x, in0=banks(4), scalar=L1.YC, in1=x,
                                               op0=ALU.mult, op1=ALU.add).then_inc(sh_add.sem, 1)

            def group(g, v):
                for j in range(SC):
                    n = g * SC + j
                    dve.wait_ge(*sh_silu.at(n + 1))
                    if not (is_static(g) and g == 0 and j < 2):
                        dve.wait_ge(*sh_lo.at(n - 1))
                    nc.vector.scalar_tensor_tensor(out=HF[:, j % 2, :GC], in0=banks(2 + j % 2),
                                                   scalar=L1.SH / (SX * SW),
                                                   in1=HA[:, (j % 2) * GC:(j % 2 + 1) * GC],
                                                   op0=ALU.mult, op1=ALU.mult).then_inc(sh_h.sem, 1)
                    dve.wait_ge(*sh_hi.at(n + 1))
                    nc.vector.tensor_tensor(HH[1][:, v, j * GC:(j + 1) * GC], HF[:, j % 2, :GC],
                                            HH[0][:, v, j * GC:(j + 1) * GC], ALU.subtract
                                            ).then_inc(sh_lo.sem, 1)
                    if j == 2 and not (is_static(g) and g == 0):
                        add(g - 1)
            stepped(dve, NG, group, 2)
            add(NG - 1)

        def blocks_sync(sp, L):
            sp.wait_ge(*rt_step.at(route_steps(L)))
            sp.wait_ge(*dp_sent.at(16 * NT * L.K))
            xs = L.xs.rearrange("(n p j) c -> p n (j c)", p=P, j=L.J)
            ys = L.ys.rearrange("(n p j) c -> p n (j c)", p=P, j=L.J)
            XC, YC = L.J * 2 * D, L.J * D

            def load(s, u):
                sp.dma_start(XG[:, u, :XC], xs[:, s, :] if is_static(s) else
                             xs[:, bass.ds(s, 1), :].rearrange("p a c -> p (a c)")).then_inc(bl_load[u].sem, 16)

            def store(s, u):
                sp.wait_ge(*bl_y.at(s + 1))
                sp.dma_start(ys[:, s, :] if is_static(s) else ys[:, bass.ds(s, 1), :].rearrange("p a c -> p (a c)"),
                             YS[:, u % 2, :YC]).then_inc(bl_st[u % 2].sem, 16)

            def step(s, u):
                if not is_static(s) or s < L.steps - 3:
                    if not (is_static(s) and s == 0):
                        sp.wait_ge(*bl_tr.at(s))
                    load(s + 3, (u + 3) % 4)
                if not is_static(s) or s >= 1:
                    store(s - 1, (u - 1) % 4)
            for s in range(3):
                load(s, s)
            stepped(sp, L.steps, step)
            store(L.steps - 1, 3)

        def blocks_tensor(pe, L):
            pe.wait_ge(*w_lo.at(len(splits)))
            pe.wait_ge(*rt_tab.at(1))
            regs = L.regs

            def transposes(s, u):
                if not is_static(s):
                    pe.wait_ge(*bl_load[u].at((s - u) // 4 * 16 + 16))
                else:
                    pe.wait_ge(*bl_load[u].at(s // 4 * 16 + 16))
                if not (is_static(s) and s < 2):
                    pe.wait_ge(*bl_xt.at(s - 1))
                bank = banks(u % 2).bitcast(F16)
                for j in range(2 * L.J):
                    ins = nc.tensor.transpose(bank[:, j * P:(j + 1) * P], XG[:, u, j * D:(j + 1) * D], IDH[:, :])
                ins.then_inc(bl_tr.sem, 1)

            def up(s, u, ex):
                pe.wait_ge(*bl_xt.at(s + 1))
                if not (is_static(s) and s < 2):
                    pe.wait_ge(*bl_h.at(s - 1))
                v = u % 2
                for j in range(L.J):
                    x = [XTB[:, v, (2 * j + h) * P:(2 * j + h + 1) * P] for h in range(2)]
                    if L is L1:
                        for b, w in ((2 + v, WG), (4 + v, WU)):
                            ins = product3(banks(b)[:, j * P:(j + 1) * P],
                                           [w[h][:, bass.ds(ex[j] * P, P)] for h in range(2)], x)
                    else:
                        for c in range(L.HC):
                            ins = product3(banks(2 + 2 * v + j)[:, c * P:(c + 1) * P],
                                           [FC[h][:, bass.ds(ex[j] * 512 + c * P, P)] for h in range(2)], x)
                ins.then_inc(bl_up.sem, 1)

            def down(s, u, ex):
                pe.wait_ge(*bl_lo.at(s + 1))
                if not (is_static(s) and s < 2):
                    pe.wait_ge(*bl_y.at(s - 1))
                v = u % 2
                w = WD if L is L1 else PJ
                for j in range(L.J):
                    for c in range(L.HC):
                        hc = (j * L.HC + c) * P
                        ins = product3(banks(6 + v)[:, j * D:(j + 1) * D],
                                       [HH[h][:, v, hc:hc + P] for h in range(2)],
                                       [w[h][:, bass.ds((ex[j] * L.HC + c) * D, D)] for h in range(2)],
                                       c == 0, c == L.HC - 1)
                ins.then_inc(bl_dn.sem, 1)

            def experts(s, u):
                r = regs[u % 2]
                src = BTAB[0:1, s * L.J:(s + 1) * L.J] if is_static(s) else BTAB[0:1, bass.ds(s * L.J, L.J)]
                nc.tensor.reg_load(r, src)
                return [nc.tensor.snap(x, min_val=0, max_val=L.E - 1) for x in r]

            held = {}

            def step(s, u):
                last = is_static(s) and s == L.steps - 1
                if not last:
                    transposes(s + 1, (u + 1) % 4)
                before = held.get("ex")
                if not is_static(s) and u == 0:
                    before = [nc.tensor.snap(x, min_val=0, max_val=L.E - 1) for x in regs[1]]
                if is_static(s) and s == L.steps - 4:
                    before = [nc.tensor.snap(x, min_val=0, max_val=L.E - 1) for x in regs[1]]
                held["ex"] = experts(s, u)
                up(s, u, held["ex"])
                if not (is_static(s) and s == 0):
                    down(s - 1, (u - 1) % 4, before)
            transposes(0, 0)
            stepped(pe, L.steps, step)
            down(L.steps - 1, 3, held["ex"])

        def blocks_scalar(act, L):
            HCOL, YCOL = L.J * L.HC * P, L.J * D

            def result(s, u):
                act.wait_ge(*bl_dn.at(s + 1))
                if not (is_static(s) and s < 2):
                    act.wait_ge(*bl_st[u % 2].at(s // 2 * 16 if is_static(s) else (s - u % 2) // 2 * 16))
                nc.scalar.activation(YS[:, u % 2, :YCOL], banks(6 + u % 2)[:, :YCOL], ACT.Copy
                                     ).then_inc(bl_y.sem, 1)

            def step(s, u):
                v = u % 2
                act.wait_ge(*bl_up.at(s + 1))
                if not (is_static(s) and s < 1):
                    act.wait_ge(*bl_h.at(s))
                if L is L1:
                    nc.scalar.activation(HA[:, :HCOL], banks(2 + v), ACT.Silu, scale=1.0 / (SX * SW)
                                         ).then_inc(bl_act.sem, 1)
                else:
                    nc.scalar.activation(HA[:, :HCOL], banks(2 + 2 * v, 2), ACT.Relu, scale=1.0 / (SX * SW)
                                         ).then_inc(bl_act.sem, 1)
                act.wait_ge(*bl_h.at(s + 1))
                if not (is_static(s) and s < 2):
                    act.wait_ge(*bl_dn.at(s - 1))
                nc.scalar.activation(HH[0][:, v, :HCOL], HF[:, v, :HCOL], ACT.Copy).then_inc(bl_hi.sem, 1)
                if not (is_static(s) and s < 1):
                    result(s - 1, (u - 1) % 4)
            stepped(act, L.steps, step)
            result(L.steps - 1, 3)

        def blocks_vector(dve, L):
            HCOL, XCOL = L.J * L.HC * P, L.J * 2 * P

            def xt(s, u):
                dve.wait_ge(*bl_tr.at(s + 1))
                if not (is_static(s) and s < 2):
                    dve.wait_ge(*bl_up.at(s - 1))
                nc.vector.tensor_copy(XTB[:, u % 2, :XCOL], banks(u % 2).bitcast(F16)[:, :XCOL]
                                      ).then_inc(bl_xt.sem, 1)

            def step(s, u):
                v = u % 2
                if not (is_static(s) and s == L.steps - 1):
                    xt(s + 1, (u + 1) % 4)
                dve.wait_ge(*bl_act.at(s + 1))
                if not (is_static(s) and s < 2):
                    dve.wait_ge(*bl_lo.at(s - 1))
                if L is L1:
                    nc.vector.scalar_tensor_tensor(out=HF[:, v, :HCOL], in0=banks(4 + v), scalar=L.SH / (SX * SW),
                                                   in1=HA[:, :HCOL], op0=ALU.mult, op1=ALU.mult
                                                   ).then_inc(bl_h.sem, 1)
                else:
                    nc.vector.scalar_tensor_tensor(out=HF[:, v, :HCOL], in0=HA[:, :HCOL], scalar=L.SH,
                                                   in1=HA[:, :HCOL], op0=ALU.mult, op1=ALU.mult
                                                   ).then_inc(bl_h.sem, 1)
                dve.wait_ge(*bl_hi.at(s + 1))
                nc.vector.tensor_tensor(HH[1][:, v, :HCOL], HF[:, v, :HCOL], HH[0][:, v, :HCOL], ALU.subtract
                                        ).then_inc(bl_lo.sem, 1)
            xt(0, 0)
            stepped(dve, L.steps, step)

        def combine_pool(pool, L):
            for u in range(2):
                pool.wait_ge(*bl_st[u].at(16 * L.steps // 2))
            GK = GT * L.K
            for g in range(NG):
                wait(pool, cb_add[g % 2], g // 2)
                for c in range(GK):
                    nc.gpsimd.indirect_dma_start(
                        out=YG[:, g % 2, c * D:(c + 1) * D], out_offset=None, in_=L.ys,
                        in_offset=bass.IndirectOffsetOnAxis(ap=ROW[:, g * GK + c:g * GK + c + 1], axis=0)
                    ).then_inc(cb_got[g % 2].sem, 16)

        def combine_vector(dve, L, last):
            GK = GT * L.K

            def moments(g, i, u):
                if not last:
                    dve.wait_ge(*cb_add[u].at(i + 1))
                    for j in range(GT):
                        statistics(g * GT + j)

            with dve.Fori(0, NG // 2) as i:
                for u in range(2):
                    g = i * 2 + u
                    dve.wait_ge(*cb_got[u].at((i + 1) * (16 * GK)))
                    if L.K == 1:
                        x = X[:, bass.ds(g * GC, GC)]
                        nc.vector.scalar_tensor_tensor(out=x, in0=YG[:, u, :GC], scalar=L.YC, in1=x, op0=ALU.mult,
                                                       op1=ALU.add).then_inc(cb_add[u].sem, 1)
                        moments(g, i, u)
                        continue
                    for k in range(L.K):
                        for j in range(GT):
                            x = X[:, bass.ds((g * GT + j) * D, D)]
                            c = j * L.K + k
                            ins = nc.vector.scalar_tensor_tensor(
                                out=x, in0=YG[:, u, c * D:(c + 1) * D],
                                scalar=W4[:, bass.ds(g * GT + j, 1), k:k + 1].rearrange("p a b -> p (a b)"),
                                in1=x, op0=ALU.mult, op1=ALU.add)
                        if k < L.K - 1:
                            ins.then_inc(cb_step.sem, 1)
                            dve.wait_ge(*cb_step.at(g * 3 + k + 1))
                    ins.then_inc(cb_add[u].sem, 1)
                    moments(g, i, u)

        bl_st = [bl_st, signal("block_stored1")]
        (b_w, b_cst, b_whi, b_wlo, b_kb, b_pstep, b_proj, b_rope, b_vhi, b_vlo, b_pack, b_ktr, b_kt, b_q1tr, b_q1,
         b_m, b_q2tr, b_q2, b_oc, b_on, b_ohi, b_olo, b_otr, b_ot, b_y, b_oadd, b_nstep, b_rstep, b_s, b_max, b_st,
         b_exp, b_phi, b_plo, b_pv) = (signal("attn1_" + n) for n in (
             "weights", "constants", "weights_hi", "weights_lo", "keys_masked", "pack_steps", "projected", "rotated",
             "v_hi", "v_lo", "packed", "k_transposed", "k_copied", "q_transposed", "q_copied", "max_written",
             "q_max_transposed", "q_max_copied", "values_copied", "values_normed", "values_hi", "values_lo",
             "values_transposed", "values_t_copied", "output", "added", "norm_steps", "rotation_steps",
             "scores_by_query", "max", "scores_by_key", "exp", "p_hi", "p_lo0", "values"))
        b_pack_k = signal("attn1_k_packed")
        b_plo = [b_plo, signal("attn1_p_lo1")]
        (a_w, a_cst, a_kv, a_kvc, a_prod, a_whi, a_wlo, a_z, a_zhi, a_zlo, a_s, a_mx, a_ex, a_nm, a_tr, a_phi, a_plo,
         a_o, a_ohi, a_olo, a_out, a_add, a_step) = (signal("attn0_" + n) for n in (
             "weights", "constants", "latent_products", "latent_products_read", "head_products", "head_hi",
             "head_lo", "z", "z_hi", "z_lo", "scores", "max", "exp", "normed", "transposed", "p_hi", "p_lo",
             "values", "values_hi", "values_lo", "projected", "added", "steps"))


        AS = BATCH * HEADS // 2
        SCALE0 = float(P) ** -0.5 / (SX * SX)

        def exists(s):
            return not is_static(s) or 0 <= s < AS

        def attn0_sync(sp):
            for dst, name in ((WQT, "wqT"), (WOH, "woh"), (WLAT[0][0:LAT], "wkdT"), (WLAT[1][0:LAT], "wvdT"),
                              (WUPS[0][0:LAT], "wku"), (WUPS[1][0:LAT], "wvu")):
                sp.dma_start(dst, a[name]).then_inc(a_w.sem, 16)

        def attn0_pool(pool):
            nc.gpsimd.memset(MASKF[:, :], 0.0).then_inc(a_cst.sem, 1)
            pool.wait_ge(*a_cst.at(1))
            nc.gpsimd.tensor_copy(IDB[:, :], IDF[:, :]).then_inc(a_cst.sem, 1)
            nc.gpsimd.affine_select(out=MASK[:, :], in_=MASKF[:, :], compare_op=ALU.is_ge, fill=-1e30, base=0,
                                    pattern=[[-1, P]], channel_multiplier=1).then_inc(a_cst.sem, 1)

        def attn0_tensor(pe):
            pe.wait_ge(*a_w.at(96))
            for n in range(2):
                for kv in range(KV):
                    ins = nc.tensor.matmul(banks(2)[:, (n * KV + kv) * D:(n * KV + kv + 1) * D],
                                           WUPS[n][0:LAT], WLAT[n][0:LAT, kv * D:(kv + 1) * D],
                                           start=True, stop=True)
            ins.then_inc(a_kv.sem, 1)
            pe.wait_ge(*a_kvc.at(1))
            for h in range(HEADS):
                kv = h // (HEADS // KV)
                hs = slice(h * D, (h + 1) * D)
                nc.tensor.matmul(banks(3 + h // 4)[:, h % 4 * D:(h % 4 + 1) * D], WQT[:, hs],
                                 WKV[0][:, kv * D:(kv + 1) * D], start=True, stop=True)
                ins = nc.tensor.matmul(banks(5 + h // 4)[:, h % 4 * D:(h % 4 + 1) * D],
                                       WKV[1][:, kv * D:(kv + 1) * D], WOH[:, hs], start=True, stop=True)
            ins.then_inc(a_prod.sem, 1)
            pe.wait_ge(*a_wlo.at(2))
            pe.wait_ge(*a_cst.at(3))
            for u in range(2):
                pe.wait_ge(*ln_xt[u].at(NG // 2))

            def xt(g, u, h, n):
                return XT[:, bass.ds(g * 2 * GC + h * GC + u // 4 * 2 * P, n)]

            def z(g, u):
                s = g * 8 + u
                if not (is_static(s) and s == 0):
                    pe.wait_ge(*a_zlo.at(s))
                for i in range(2):
                    h = u % 4 * 2 + i
                    ins = product3(banks(0)[:, i * 256:(i + 1) * 256],
                                   [AH[n][:, h * D:(h + 1) * D] for n in range(2)],
                                   [xt(g, u, n, 256) for n in range(2)])
                ins.then_inc(a_z.sem, 1)

            def scores(g, u):
                s = g * 8 + u
                pe.wait_ge(*a_zlo.at(s + 1))
                if not (is_static(s) and s == 0):
                    pe.wait_ge(*a_ex.at(s))
                for i in range(2):
                    for q in range(2):
                        at = q * P
                        nc_, first = (q + 1) * P, q * P
                        zq = [ZB[n][:, s_par(u), i * 256 + at:i * 256 + at + P] for n in range(2)]
                        o = banks(1 + i)[:, at:at + nc_]
                        x = [xt(g, u, n, nc_) for n in range(2)]
                        nc.tensor.matmul(o, zq[0], x[0], start=True, stop=False)
                        nc.tensor.matmul(o, zq[0], x[1], start=False, stop=False)
                        nc.tensor.matmul(o, zq[1], x[0], start=False, stop=False)
                        ins = nc.tensor.matmul(banks(1 + i)[:, at + first:at + first + P], IDB[:, :], MASK[:, :],
                                               start=False, stop=True)
                ins.then_inc(a_s.sem, 1)

            def transposes(g, u):
                s = g * 8 + u
                pe.wait_ge(*a_nm.at(s + 1))
                if not (is_static(s) and s == 0):
                    pe.wait_ge(*a_plo.at(s))
                for i in range(2):
                    for c in range(3):
                        ins = nc.tensor.transpose(banks(3 + i)[:, c * P:(c + 1) * P],
                                                  PF[:, s_par(u), (i * 3 + c) * P:(i * 3 + c + 1) * P], IDF[:, :])
                ins.then_inc(a_tr.sem, 1)

            def values(g, u):
                s = g * 8 + u
                pe.wait_ge(*a_plo.at(s + 1))
                if not (is_static(s) and s == 0):
                    pe.wait_ge(*a_olo.at(s))
                t = g * 4 + u // 4 * 2
                for i in range(2):
                    for k in range(2):
                        x = [XH[:, bass.ds(((t + k) * 2 + n) * D, D)] for n in range(2)]
                        c = i * 3 * P + k * 2 * P
                        w = (2 - k) * P
                        ins = product3(banks(5)[:, i * 256 + k * P:i * 256 + k * P + w], x,
                                       [PTB[n][:, s_par(u), c:c + w] for n in range(2)], k == 0, k == 1)
                ins.then_inc(a_o.sem, 1)

            def project(g, u):
                s = g * 8 + u
                pe.wait_ge(*a_olo.at(s + 1))
                b = g * 2 + u // 4
                if u % 4 == 0 and not (is_static(b) and b < 2):
                    pe.wait_ge(*a_add.at(b - 1))
                for i in range(2):
                    h = u % 4 * 2 + i
                    for q in range(2):
                        ins = product3(banks(6 + u // 4)[:, q * D:(q + 1) * D],
                                       [OB[n][:, s_par(u), i * 256 + q * P:i * 256 + (q + 1) * P] for n in range(2)],
                                       [BH[n][:, h * D:(h + 1) * D] for n in range(2)],
                                       h == 0 and q == 0, h == HEADS - 1, skip_group_check=True)
                ins.then_inc(a_out.sem, 1)

            def step(g, u):
                s = g * 8 + u
                if exists(s + 2):
                    z(*back(g, u, -2))
                if exists(s + 1):
                    scores(*back(g, u, -1))
                if exists(s):
                    transposes(g, u)
                if exists(s - 1):
                    values(*back(g, u, 1))
                if exists(s - 2):
                    project(*back(g, u, 2))
            attention_steps(pe, step)

        def s_par(u):
            return u % 2

        def back(g, u, n):
            return g + (u - n) // 8, (u - n) % 8

        def attention_steps(eng, step):
            for u in range(-2, 8):
                step(0, u)
            with eng.Fori(1, AS // 8 - 1) as g:
                for u in range(8):
                    step(g, u)
            for u in range(8):
                step(AS // 8 - 1, u)
            for u in range(3):
                step(AS // 8, u)

        def attn0_scalar(act):
            act.wait_ge(*a_kv.at(1))
            for n in range(2):
                ins = nc.scalar.activation(WKV[n][:, :], banks(2)[:, n * KV * D:(n + 1) * KV * D], ACT.Copy)
            ins.then_inc(a_kvc.sem, 1)
            act.wait_ge(*a_prod.at(1))
            for n, w in enumerate((AH, BH)):
                nc.scalar.activation(w[0][:, :], banks(3 + 2 * n, 2), ACT.Copy, scale=SW).then_inc(a_whi.sem, 1)

            def zhi(g, u):
                s = g * 8 + u
                act.wait_ge(*a_z.at(s + 1))
                if not (is_static(s) and s < 2):
                    act.wait_ge(*a_s.at(s - 1))
                nc.scalar.activation(ZB[0][:, s_par(u), :], banks(0), ACT.Copy, scale=1.0 / SW
                                     ).then_inc(a_zhi.sem, 1)

            def exp(g, u):
                s = g * 8 + u
                act.wait_ge(*a_mx.at(s + 1))
                if not (is_static(s) and s < 2):
                    act.wait_ge(*a_tr.at(s - 1))
                for i in range(2):
                    for q in range(2):
                        o = PF[:, s_par(u), (i * 3 + q) * P:(i * 3 + 2 * q + 1) * P]
                        ins = nc.scalar.activation(o, banks(1 + i)[:, q * P:(2 * q + 1) * P], ACT.Exp,
                                                   bias=NM[:, s_par(u), i * 2 + q:i * 2 + q + 1], scale=SCALE0,
                                                   accum_out=RS[:, s_par(u), i * 2 + q:i * 2 + q + 1])
                ins.then_inc(a_ex.sem, 1)

            def phi(g, u):
                s = g * 8 + u
                act.wait_ge(*a_tr.at(s + 1))
                if not (is_static(s) and s < 2):
                    act.wait_ge(*a_o.at(s - 1))
                nc.scalar.activation(PTB[0][:, s_par(u), :].rearrange("p (i c) -> p i c", i=2),
                                     PS[:, 3:5, 0:3 * P], ACT.Copy, scale=SP).then_inc(a_phi.sem, 1)

            def ohi(g, u):
                s = g * 8 + u
                act.wait_ge(*a_o.at(s + 1))
                if not (is_static(s) and s < 2):
                    act.wait_ge(*a_out.at(s - 1))
                nc.scalar.activation(OB[0][:, s_par(u), :], banks(5), ACT.Copy, scale=1.0 / SP
                                     ).then_inc(a_ohi.sem, 1)

            def step(g, u):
                s = g * 8 + u
                if exists(s - 1):
                    phi(*back(g, u, 1))
                if exists(s):
                    exp(g, u)
                if exists(s + 2):
                    zhi(*back(g, u, -2))
                if exists(s - 2):
                    ohi(*back(g, u, 2))
            attention_steps(act, step)

        def attn0_vector(dve, last):
            for n, w in enumerate((AH, BH)):
                dve.wait_ge(*a_whi.at(n + 1))
                nc.vector.scalar_tensor_tensor(out=w[1][:, :], in0=banks(3 + 2 * n, 2), scalar=SW, in1=w[0][:, :],
                                               op0=ALU.mult, op1=ALU.subtract).then_inc(a_wlo.sem, 1)

            def zlo(g, u):
                s = g * 8 + u
                dve.wait_ge(*a_zhi.at(s + 1))
                nc.vector.scalar_tensor_tensor(out=ZB[1][:, s_par(u), :], in0=banks(0), scalar=1.0 / SW,
                                               in1=ZB[0][:, s_par(u), :], op0=ALU.mult, op1=ALU.subtract
                                               ).then_inc(a_zlo.sem, 1)

            def row_max(g, u):
                s = g * 8 + u
                dve.wait_ge(*a_s.at(s + 1))
                if not (is_static(s) and s < 2):
                    dve.wait_ge(*a_ex.at(s - 1))
                nm = NM[:, s_par(u), :].rearrange("p (i q) -> p i q", q=2)
                nc.vector.reduce_max(nm[:, :, 0], PS[:, 1:3, 0:P], axis=AX.X)
                nc.vector.reduce_max(nm[:, :, 1], PS[:, 1:3, P:3 * P], axis=AX.X).then_inc(a_step.sem, 1)
                dve.wait_ge(*a_step.at(2 * s + 1))
                nc.vector.tensor_scalar(NM[:, s_par(u), :], NM[:, s_par(u), :], -SCALE0, None, ALU.mult
                                        ).then_inc(a_mx.sem, 1)

            def norm(g, u):
                s = g * 8 + u
                dve.wait_ge(*a_ex.at(s + 1))
                nc.vector.reciprocal(RS[:, s_par(u), :], RS[:, s_par(u), :]).then_inc(a_step.sem, 1)
                dve.wait_ge(*a_step.at(2 * s + 2))
                for i in range(2):
                    for q in range(2):
                        o = PF[:, s_par(u), (i * 3 + q) * P:(i * 3 + 2 * q + 1) * P]
                        ins = nc.vector.tensor_scalar(o, o, RS[:, s_par(u), i * 2 + q:i * 2 + q + 1], None, ALU.mult)
                ins.then_inc(a_nm.sem, 1)

            def plo(g, u):
                s = g * 8 + u
                dve.wait_ge(*a_phi.at(s + 1))
                two = "p (i c) -> p i c"
                nc.vector.scalar_tensor_tensor(out=PTB[1][:, s_par(u), :].rearrange(two, i=2),
                                               in0=PS[:, 3:5, 0:3 * P], scalar=SP,
                                               in1=PTB[0][:, s_par(u), :].rearrange(two, i=2),
                                               op0=ALU.mult, op1=ALU.subtract).then_inc(a_plo.sem, 1)

            def olo(g, u):
                s = g * 8 + u
                dve.wait_ge(*a_ohi.at(s + 1))
                nc.vector.scalar_tensor_tensor(out=OB[1][:, s_par(u), :], in0=banks(5), scalar=1.0 / SP,
                                               in1=OB[0][:, s_par(u), :], op0=ALU.mult, op1=ALU.subtract
                                               ).then_inc(a_olo.sem, 1)

            def add(g, u):
                dve.wait_ge(*a_out.at(g * 8 + u + 1))
                x = X[:, bass.ds((g * 2 + u // 4) * 2 * D, 2 * D)]
                nc.vector.scalar_tensor_tensor(out=x, in0=banks(6 + u // 4)[:, 0:2 * D], scalar=1.0 / (SX * SW),
                                               in1=x, op0=ALU.mult, op1=ALU.add).then_inc(a_add.sem, 1)
                if not last:
                    dve.wait_ge(*a_add.at(g * 2 + u // 4 + 1))
                    for j in range(2):
                        statistics((g * 2 + u // 4) * 2 + j)

            def step(g, u):
                s = g * 8 + u
                if exists(s):
                    row_max(g, u)
                if exists(s + 1):
                    zlo(*back(g, u, -1))
                if exists(s - 1):
                    plo(*back(g, u, 1))
                if exists(s):
                    norm(g, u)
                if exists(s - 2):
                    olo(*back(g, u, 2))
                if u % 4 == 2 and exists(s - 3):
                    add(*back(g, u, 3))
            attention_steps(dve, step)

        ATTN0_COUNTS = {a_w: 96, a_cst: 3, a_kv: 1, a_kvc: 1, a_prod: 1, a_whi: 2, a_wlo: 2, a_add: BATCH,
                        a_step: 2 * AS}
        ATTN0_COUNTS.update({s: AS for s in (a_z, a_zhi, a_zlo, a_s, a_mx, a_ex, a_nm, a_tr, a_phi, a_plo, a_o,
                                             a_ohi, a_olo, a_out)})

        MSCALE = 2.0 ** 14
        SCALE1 = float(D) ** -0.5 / (SX * SX)
        bank1 = banks(1).bitcast(F16)
        KB = [w[:, :].rearrange("p (r k) -> p r k", r=4) for w in (*FC, *PJ)]

        def wait_split(eng, i, c, g):
            wait(eng, b_plo[g % 2], 2 * (i * 8 + c) + g // 2 + 1)

        def tile_exists(i, c):
            return not is_static(i) or 0 <= c < NT

        def tile_turns(eng, turn):
            for c in range(-5, 3):
                turn(0, c)
            with eng.Fori(0, (NT - 8) // 8) as i:
                for c in range(3, 11):
                    turn(i, c)
            for c in range(NT - 5, NT + 2):
                turn(0, c)

        def attn1_sync(sp):
            for dst, name in ((WST[:, 0:352], "aqkv"), (WST[:, 352:], "awo"),
                              (COS[:, :, :], "acos"), (SIN[:, :, :], "asin")):
                sp.dma_start(dst, a[name]).then_inc(b_w.sem, 16)

        def attn1_pool(pool):
            pool.wait_ge(*ln_lo.at(NG))
            for n, (buf, v) in enumerate([(q[:, :, :], 0.0) for q in QP] + [(KP[:, :, :, :], 0.0),
                                                                            (MASKR[:, :], 1.0), (LNSP, LOGSP)]):
                nc.gpsimd.memset(buf, v).then_inc(b_cst.sem, 1)
            ones = VP[:, :, :].rearrange("p t (g c) -> p t g c", c=17)[:, :, :, 8]
            nc.gpsimd.memset(ones, 1.0).then_inc(b_cst.sem, 1)
            pool.wait_ge(*b_cst.at(8))
            nc.gpsimd.memset(KP[:, :, :, 24], MSCALE).then_inc(b_cst.sem, 1)
            nc.gpsimd.affine_select(out=MASKR[:, :], in_=MASKR[:, :], compare_op=ALU.is_ge, fill=0.0, base=0,
                                    pattern=[[-32, 4]], channel_multiplier=1).then_inc(b_cst.sem, 1)
            pool.wait_ge(*b_cst.at(10))
            nc.gpsimd.affine_select(out=MASKR[:, :], in_=MASKR[:, :], compare_op=ALU.is_ge, fill=0.0, base=31,
                                    pattern=[[32, 4]], channel_multiplier=-1).then_inc(b_cst.sem, 1)
            pool.wait_ge(*b_cst.at(11))

            def pack_k(i, c):
                t = i * 8 + c
                wait(pool, b_rope, t + 1)
                wait(pool, b_ktr, t)
                carry_wait()
                k8 = RF[:, c % 2, P:160].rearrange("p (g c) -> p g c", c=8).unsqueeze(2).to_broadcast([P, 4, 4, 8])
                nc.gpsimd.tensor_copy(KP[:, :, :, 0:8], k8)
                nc.gpsimd.tensor_copy(KP[:, :, :, 16:24], k8).then_inc(b_pstep.sem, 1)
                wait(pool, b_pstep, 2 * t + 1)
                nc.gpsimd.tensor_tensor(KP[:, :, :, 8:16], k8, KP[:, :, :, 0:8], ALU.subtract
                                        ).then_inc(b_pack_k.sem, 1)

            def pack_q(i, c):
                t = i * 8 + c
                wait(pool, b_q2tr, t - 3)
                carry_wait()
                q8, qp = RF[:, c % 2, 0:P].rearrange("p (h c) -> p h c", c=8), QP[c % 4]
                nc.gpsimd.memset(qp[:, :, 24], 0.0)
                nc.gpsimd.tensor_copy(qp[:, :, 0:8], q8)
                nc.gpsimd.tensor_copy(qp[:, :, 8:16], q8).then_inc(b_pstep.sem, 1)
                wait(pool, b_pstep, 2 * t + 2)
                nc.gpsimd.tensor_tensor(qp[:, :, 16:24], q8, qp[:, :, 0:8], ALU.subtract).then_inc(b_pack.sem, 1)

            def plo(i, c, g):
                wait(pool, b_phi, 4 * (i * 8 + c) + g + 1)
                nc.gpsimd.tensor_tensor(PB1[1][:, g, :], PF1[:, g, :], PB1[0][:, g, :],
                                        ALU.subtract).then_inc(b_plo[1].sem, 1)

            def turn(i, c):
                if tile_exists(i, c + 4):
                    pack_k(i, c + 4)
                if tile_exists(i, c - 1):
                    plo(i, c - 1, 3)
                if tile_exists(i, c + 4):
                    pack_q(i, c + 4)
                if tile_exists(i, c):
                    plo(i, c, 1)
            tile_turns(pool, turn)

        def attn1_tensor(pe):
            pe.wait_ge(*b_wlo.at(2))
            pe.wait_ge(*b_cst.at(11))
            for u in range(2):
                pe.wait_ge(*ln_xt[u].at(NG // 2))

            def scores(i, c, g):
                t = i * 8 + c
                wait(pe, b_q1, t + 1)
                wait(pe, b_kb, (i * 4 + c // 2) * 2 + 2)
                wait(pe, b_max, 4 * t + g)
                for rr in range(2):
                    ins = nc.tensor.matmul(banks(2 + rr), QT1[:, c % 2, g * P:(g + 1) * P],
                                           KB[c // 2 % 4][:, 2 * rr:2 * rr + 2, g * 256:(g + 1) * 256],
                                           start=True, stop=True)
                ins.then_inc(b_s.sem, 1)

            def by_key(i, c, g):
                t = i * 8 + c
                wait(pe, b_q2, t + 1)
                wait(pe, b_exp, 4 * t + g)
                for k in range(2):
                    for r in range(4):
                        ins = nc.tensor.matmul(banks(4 + k)[:, r * P:(r + 1) * P],
                                               KB[c // 2 % 4][:, r, g * 256 + k * P:g * 256 + (k + 1) * P],
                                               QT2[:, c % 2, g * P:(g + 1) * P], start=True, stop=True)
                ins.then_inc(b_st.sem, 1)

            def values(i, c, g):
                t = i * 8 + c
                wait_split(pe, i, c, g)
                if g == 0:
                    wait(pe, b_oc, t)
                for r in range(4):
                    o = (4 * g + r) * 17
                    for k in range(2):
                        v = VP[:, bass.ds(i * 8 + c // 2 * 2 + k, 1), g * 17:(g + 1) * 17].rearrange("p a c -> p (a c)")
                        p = [PB1[n][:, g, (k * 4 + r) * P:(k * 4 + r + 1) * P] for n in range(2)]
                        nc.tensor.matmul(banks(6)[:, o:o + 17], p[0], v, start=k == 0, stop=False)
                        ins = nc.tensor.matmul(banks(6)[:, o:o + 9], p[1], v[:, 0:9], start=False, stop=k == 1)
                ins.then_inc(b_pv.sem, 1)

            def project(i, c):
                t = i * 8 + c
                wait(pe, b_vlo, t)
                x = [XT[:, bass.ds((i * 2 + c // 4) * 2 * GC + n * GC + c % 4 * P, P)] for n in range(2)]
                product3(banks(0)[:, 0:352], x, [AW[n][:, :] for n in range(2)]).then_inc(b_proj.sem, 1)

            def four(src, sig):
                for g in range(4):
                    ins = nc.tensor.transpose(bank1[:, g * P:(g + 1) * P], src(g), IDH[:, :])
                ins.then_inc(sig.sem, 1)

            def q_four(c, sig):
                four(lambda g: QP[c % 4][:, 4 * g:4 * g + 4, :].rearrange("p r c -> p (r c)"), sig)

            def turn(i, c):
                t = i * 8 + c
                for g in range(4):
                    if tile_exists(i, c):
                        by_key(i, c, g)
                    if tile_exists(i, c + 2):
                        scores(i, c + 2, g)
                    before = c - 1 if g < 3 else c
                    if tile_exists(i, before):
                        values(i, before, (g - 3) % 4)
                    if g == 0 and tile_exists(i, c + 1):
                        wait(pe, b_m, t + 2)
                        wait(pe, b_q1, t + 3 if tile_exists(i, c + 2) else NT)
                        wait(pe, b_q2, t + 1)
                        q_four(c + 1, b_q2tr)
                    if g == 1 and tile_exists(i, c - 2):
                        wait(pe, b_olo, t - 1)
                        wait(pe, b_oadd, t - 2)
                        for n in range(2):
                            ins = nc.tensor.transpose(banks(7).bitcast(F16)[:, n * P:(n + 1) * P], ONB[n][:, :],
                                                      IDH[:, :])
                        ins.then_inc(b_otr.sem, 1)
                    if g == 1 and tile_exists(i, c + 4):
                        wait(pe, b_pack_k, t + 5)
                        if tile_exists(i, c + 1):
                            wait(pe, b_q2, t + 2)
                        else:
                            wait(pe, b_q1, t + 3)
                        four(lambda g: KP[:, g, :, :].rearrange("p r c -> p (r c)"), b_ktr)
                    if g == 2 and tile_exists(i, c + 5):
                        project(i, c + 5)
                    if g == 2 and tile_exists(i, c + 3):
                        wait(pe, b_pack, t + 4)
                        if tile_exists(i, c + 4):
                            wait(pe, b_kt, t + 5)
                        else:
                            wait(pe, b_q2, t + 2)
                        q_four(c + 3, b_q1tr)
                    if g == 3 and tile_exists(i, c - 2):
                        wait(pe, b_ot, t - 1)
                        product3(banks(7)[:, 0:D], [OTB[:, n * P:(n + 1) * P] for n in range(2)],
                                 [AO[n][:, :] for n in range(2)]).then_inc(b_y.sem, 1)
            tile_turns(pe, turn)

        def attn1_scalar(act):
            act.wait_ge(*b_w.at(64))
            for n, (w, c, m) in enumerate(((AW, 0, 352), (AO, 352, P))):
                nc.scalar.activation(w[0][:, :], WST[:, c:c + m], ACT.Copy, scale=SW).then_inc(b_whi.sem, 1)
            act.wait_ge(*b_cst.at(11))

            def exp(i, c, g):
                n = 4 * (i * 8 + c) + g
                wait(act, b_st, n + 1)
                if tile_exists(i, c - 1):
                    wait_split(act, i, c - 1, g)
                nc.scalar.activation(PF1[:, g, :], banks(4, 2), ACT.Exp, bias=LNSP[:, 0:1],
                                     scale=SCALE1).then_inc(b_exp.sem, 1)

            def phi(i, c, g):
                n = 4 * (i * 8 + c) + g
                wait(act, b_exp, n + 1)
                wait(act, b_pv, n - 3)
                nc.scalar.activation(PB1[0][:, g, :], PF1[:, g, :], ACT.Copy).then_inc(b_phi.sem, 1)

            def turn(i, c):
                t = i * 8 + c
                for g in range(4):
                    if tile_exists(i, c):
                        exp(i, c, g)
                    if g == 0 and tile_exists(i, c - 2):
                        wait(act, b_on, t - 1)
                        wait(act, b_otr, t - 2)
                        nc.scalar.activation(ONB[0][:, :], ON[:, :, :].rearrange("p h c -> p (h c)"), ACT.Copy
                                             ).then_inc(b_ohi.sem, 1)
                    if g == 2 and tile_exists(i, c + 4):
                        wait(act, b_ktr, t + 5)
                        wait(act, b_kb, t + 3)
                        nc.scalar.activation(KTB[:, c % 2, :], bank1[:, 0:512], ACT.Copy).then_inc(b_kt.sem, 1)
                    if g == 3 and tile_exists(i, c - 1):
                        wait(act, b_pv, 4 * t)
                        wait(act, b_on, t - 1)
                        nc.scalar.activation(OS[:, :], banks(6)[:, 0:272], ACT.Copy).then_inc(b_oc.sem, 1)
                    if g == 3 and tile_exists(i, c + 5):
                        wait(act, b_proj, t + 6)
                        v = VP[:, bass.ds(t + 5, 1), :].rearrange("p t (g c) -> p (t g) c", c=17)
                        nc.scalar.activation(v[:, :, 0:8], banks(0)[:, 320:352].rearrange("p (g c) -> p g c", c=8),
                                             ACT.Copy, scale=1.0 / SW).then_inc(b_vhi.sem, 1)
                    if g == 3 and tile_exists(i, c + 3):
                        wait(act, b_q1tr, t + 4)
                        wait(act, b_s, 4 * t + 8)
                        nc.scalar.activation(QT1[:, (c + 3) % 2, :], bank1[:, 0:512], ACT.Copy
                                             ).then_inc(b_q1.sem, 1)
                    before = c - 1 if g < 1 else c
                    if tile_exists(i, before):
                        phi(i, before, (g - 1) % 4)
            tile_turns(act, turn)

        def attn1_vector(dve, last):
            for n, (w, c, m) in enumerate(((AW, 0, 352), (AO, 352, P))):
                dve.wait_ge(*b_whi.at(n + 1))
                nc.vector.scalar_tensor_tensor(out=w[1][:, :], in0=WST[:, c:c + m], scalar=SW, in1=w[0][:, :],
                                               op0=ALU.mult, op1=ALU.subtract).then_inc(b_wlo.sem, 1)
            dve.wait_ge(*b_cst.at(11))

            def rope(i, c):
                t = i * 8 + c
                wait(dve, b_vhi, t + 1)
                wait(dve, b_pack, t - 1)
                wait(dve, b_rope, t)
                nc.vector.scalar_tensor_tensor(out=RT[:, 0, :], in0=banks(0)[:, 0:160], scalar=1.0 / SW,
                                               in1=COS[:, c % 2, :], op0=ALU.mult, op1=ALU.mult)
                nc.vector.scalar_tensor_tensor(out=RT[:, 1, :], in0=banks(0)[:, 160:320], scalar=1.0 / SW,
                                               in1=SIN[:, c % 2, :], op0=ALU.mult, op1=ALU.mult
                                               ).then_inc(b_rstep.sem, 1)
                vp = VP[:, bass.ds(t, 1), :].rearrange("p t (g c) -> p (t g) c", c=17)
                nc.vector.scalar_tensor_tensor(out=vp[:, :, 9:17],
                                               in0=banks(0)[:, 320:352].rearrange("p (g c) -> p g c", c=8),
                                               scalar=1.0 / SW, in1=vp[:, :, 0:8], op0=ALU.mult,
                                               op1=ALU.subtract).then_inc(b_vlo.sem, 1)
                wait(dve, b_rstep, t + 1)
                nc.vector.tensor_tensor(RF[:, c % 2, :], RT[:, 0, :], RT[:, 1, :], ALU.add).then_inc(b_rope.sem, 1)

            def masks(i, c):
                wait(dve, b_kt, i * 8 + c + 1)
                wait(dve, b_st, 4 * (2 * (i * 4 + c // 2) - 5))
                kb = KB[c // 2 % 4].rearrange("p r (g k) -> p r g k", g=4)
                for r in range(4):
                    ins = nc.vector.tensor_scalar(kb[:, r, :, c % 2 * P:(c % 2 + 1) * P],
                                                  KTB[:, c % 2, :].rearrange("p (g k) -> p g k", g=4),
                                                  MASKR[:, r:r + 1], None, ALU.mult)
                ins.then_inc(b_kb.sem, 1)

            def plo(i, c, g):
                wait(dve, b_phi, 4 * (i * 8 + c) + g + 1)
                nc.vector.tensor_tensor(PB1[1][:, g, :], PF1[:, g, :], PB1[0][:, g, :],
                                        ALU.subtract).then_inc(b_plo[0].sem, 1)

            def norm(i, c):
                t = i * 8 + c
                wait(dve, b_oc, t + 1)
                os = OS[:, :].rearrange("p (h c) -> p h c", c=17)
                nc.vector.tensor_tensor(ON[:, :, :], os[:, :, 0:8], os[:, :, 9:17], ALU.add)
                nc.vector.reciprocal(RC[:, :], os[:, :, 8]).then_inc(b_nstep.sem, 1)
                wait(dve, b_nstep, t + 1)
                nc.vector.tensor_tensor(ON[:, :, :], ON[:, :, :], RC[:, :].unsqueeze(2).to_broadcast([P, 16, 8]),
                                        ALU.mult).then_inc(b_on.sem, 1)

            def turn(i, c):
                t = i * 8 + c
                if tile_exists(i, c + 1):
                    wait(dve, b_max, 4 * t + 8)
                    wait(dve, b_q1tr, t + 2)
                    nc.vector.tensor_scalar(QP[(c + 1) % 4][:, :, 24], MX[:, (c + 1) % 2, :], -1.0 / MSCALE, None,
                                            ALU.mult).then_inc(b_m.sem, 1)
                for g in range(4):
                    if tile_exists(i, c + 2):
                        wait(dve, b_s, 4 * t + g + 9)
                        nc.vector.reduce_max(MX[:, c % 2, 4 * g:4 * g + 4],
                                             PS[:, 2:4, :].rearrange("p b (r k) -> p (b r) k", k=256), axis=AX.X
                                             ).then_inc(b_max.sem, 1)
                    if g == 1 and tile_exists(i, c):
                        plo(i, c, 0)
                    if g == 0 and tile_exists(i, c + 1):
                        wait(dve, b_q2tr, t + 2)
                        wait(dve, b_st, 4 * t)
                        nc.vector.tensor_copy(QT2[:, (c + 1) % 2, :], bank1[:, 0:512]).then_inc(b_q2.sem, 1)
                    if g == 0 and tile_exists(i, c - 2):
                        wait(dve, b_ohi, t - 1)
                        nc.vector.tensor_tensor(ONB[1][:, :], ON[:, :, :].rearrange("p h c -> p (h c)"),
                                                ONB[0][:, :], ALU.subtract).then_inc(b_olo.sem, 1)
                    if g == 0 and tile_exists(i, c - 1):
                        plo(i, c - 1, 2)
                    if g == 2 and tile_exists(i, c - 2):
                        wait(dve, b_otr, t - 1)
                        wait(dve, b_y, t - 2)
                        nc.vector.tensor_copy(OTB[:, :], banks(7).bitcast(F16)[:, 0:2 * P]).then_inc(b_ot.sem, 1)
                    if g == 2 and tile_exists(i, c + 4):
                        masks(i, c + 4)
                    if g == 1 and not last and tile_exists(i, c - 3):
                        wait(dve, b_oadd, t - 2)
                        statistics(t - 3)
                    if g == 3 and tile_exists(i, c + 5):
                        rope(i, c + 5)
                    if g == 3 and tile_exists(i, c - 1):
                        wait(dve, b_olo, t - 1)
                        norm(i, c - 1)
                    if g == 3 and tile_exists(i, c - 2):
                        wait(dve, b_y, t - 1)
                        x = X[:, bass.ds((t - 2) * D, D)]
                        nc.vector.scalar_tensor_tensor(out=x, in0=banks(7)[:, 0:D], scalar=1.0 / (SX * SW), in1=x,
                                                       op0=ALU.mult, op1=ALU.add).then_inc(b_oadd.sem, 1)
            tile_turns(dve, turn)
            if not last:
                dve.wait_ge(*b_oadd.at(NT))
                statistics(NT - 1)

        ATTN1_COUNTS = {b_w: 64, b_cst: 11, b_whi: 2, b_wlo: 2, b_kb: NT, b_pack_k: NT, b_pstep: 2 * NT}
        ATTN1_COUNTS.update({s: NT for s in (b_proj, b_rope, b_vhi, b_vlo, b_pack, b_ktr, b_kt, b_q1tr, b_q1, b_m,
                                             b_q2tr, b_q2, b_oc, b_on, b_ohi, b_olo, b_otr, b_ot, b_y, b_oadd,
                                             b_nstep, b_rstep)})
        ATTN1_COUNTS.update({s: 4 * NT for s in (b_s, b_max, b_st, b_exp, b_phi, b_pv)})
        ATTN1_COUNTS.update({s: 2 * NT for s in b_plo})

        def moe_counts(L):
            g = NG // 2
            c = {logits: NG, rt_step: route_steps(L), rt_choice: 1, rt_pos: 1, rt_bex: 1, rt_brow: 1, rt_tab: 1,
                 rt_row: 1, dp_sent: 16 * NT * L.K, bl_tr: L.steps, bl_xt: L.steps, bl_up: L.steps, bl_act: L.steps,
                 bl_h: L.steps, bl_hi: L.steps, bl_lo: L.steps, bl_dn: L.steps, bl_y: L.steps}
            for u in range(2):
                c.update({bl_st[u]: 8 * L.steps, cb_got[u]: 16 * GT * L.K * g,
                          cb_add[u]: g})
            for u in range(4):
                c[bl_load[u]] = 4 * L.steps
            if L is L1:
                c.update({rt_shift: 2, rt_exp: 2, sh_gu: NT, sh_silu: NT, sh_h: NT, sh_hi: NT, sh_lo: NT,
                          sh_y: NG, sh_add: NG, cb_step: 3 * NG})
            return c

        def counts(ph):
            c = dict(LN_COUNTS)
            if ph in ("moe0", "moe1"):
                c.update(moe_counts(L0 if ph == "moe0" else L1))
            if ph == "attn0":
                c.update(ATTN0_COUNTS)
            if ph == "attn1":
                c.update(ATTN1_COUNTS)
            return c

        every = [s for s in {**LN_COUNTS, **moe_counts(L0), **moe_counts(L1), **ATTN0_COUNTS,
                               **ATTN1_COUNTS}]

        def each_phase(run):
            for s in every:
                s.base = 0
            ready = [(x_loaded.sem, 16)]
            for n, ph in enumerate(phases):
                run(ph, ready, n == 0, n == len(phases) - 1)
                for s, n in counts(ph).items():
                    s.base += n
                if ph in ("moe0", "moe1"):
                    ready = [(cb_add[u].sem, cb_add[u].base) for u in range(2)]
                if ph == "attn0":
                    ready = [(a_add.sem, a_add.base)]
                if ph == "attn1":
                    ready = [(b_oadd.sem, b_oadd.base)]
            return ready

        block = ctx.enter_context(nc.Block())

        @block.sync
        def _(sp):
            setup_sync(sp)

            def run(ph, ready, first, last):
                if ph in ("moe0", "moe1"):
                    blocks_sync(sp, L0 if ph == "moe0" else L1)
                if ph == "attn0":
                    sp.wait_ge(*ln_lo.at(NG))
                    attn0_sync(sp)
                    zero_slots(sp, L1)
                if ph == "attn1":
                    sp.wait_ge(*ln_lo.at(NG))
                    attn1_sync(sp)
            ready = each_phase(run)
            for s, n in ready:
                sp.wait_ge(s, n)
            sp.dma_start(out.rearrange("(t p) d -> p t d", p=P),
                         X[:, :].rearrange("p (t d) -> p t d", d=D)).then_inc(written.sem, 16)
            sp.wait_ge(*written.at(16))

        @block.gpsimd
        def _(pool):
            setup_pool(pool)

            def run(ph, ready, first, last):
                ln_pool(pool)
                if ph in ("moe0", "moe1"):
                    L = L0 if ph == "moe0" else L1
                    dispatch_pool(pool, L)
                    combine_pool(pool, L)
                if ph == "attn0":
                    pool.wait_ge(*ln_lo.at(NG))
                    attn0_pool(pool)
                if ph == "attn1":
                    attn1_pool(pool)
            each_phase(run)

        @block.scalar
        def _(act):
            split_scalar(act, 0, FIRST)

            def run(ph, ready, first, last):
                for s, n in ready:
                    act.wait_ge(s, n)
                ln_scalar(act)
                if ph in ("moe0", "moe1"):
                    L = L0 if ph == "moe0" else L1
                    route_scalar(act, L)
                if first:
                    split_scalar(act, FIRST, len(splits))
                if ph in ("moe0", "moe1"):
                    if L is L1:
                        act.wait_ge(*rt_row.at(1))
                        shared_scalar(act)
                    blocks_scalar(act, L)
                if ph == "attn0":
                    attn0_scalar(act)
                if ph == "attn1":
                    attn1_scalar(act)
            each_phase(run)

        @block.vector
        def _(dve):
            nc.vector.memset(ZERO[:, :], 0.0).then_inc(zeros.sem, 1)
            split_vector(dve, 0, FIRST)

            def run(ph, ready, first, last):
                for s, n in ready:
                    dve.wait_ge(s, n)
                ln_vector(dve, first)
                if ph in ("moe0", "moe1"):
                    L = L0 if ph == "moe0" else L1
                    route_vector(dve, L)
                if first:
                    split_vector(dve, FIRST, len(splits))
                if ph in ("moe0", "moe1"):
                    if L is L1:
                        shared_vector(dve)
                    blocks_vector(dve, L)
                    combine_vector(dve, L, last)
                if ph == "attn0":
                    attn0_vector(dve, last)
                if ph == "attn1":
                    attn1_vector(dve, last)
            each_phase(run)

        @block.tensor
        def _(pe):
            for L in (L0, L1):
                L.regs = [[pe.alloc_register(f"{L.tag}_expert{u}_{j}") for j in range(L.J)] for u in range(2)]

            def run(ph, ready, first, last):
                for s, n in ready:
                    pe.wait_ge(s, n)
                ln_tensor(pe, {"moe0": L0, "moe1": L1}.get(ph))
                if ph in ("moe0", "moe1"):
                    L = L0 if ph == "moe0" else L1
                    route_tensor(pe, L)
                    if L is L1:
                        shared_tensor(pe)
                    blocks_tensor(pe, L)
                if ph == "attn0":
                    attn0_tensor(pe)
                if ph == "attn1":
                    attn1_tensor(pe)
            each_phase(run)


INS = ["x", "fc", "pj", "rw0", "wg", "wu", "wd", "sg", "su", "sd", "rw1", "bias", "wqT", "woh", "wkdT", "wvdT", "wku", "wvu",
       "aqkv", "awo", "acos", "asin"]


def rotation():
    inv = (1.0 / np.float32(10000.0) ** (np.arange(0, D, 2, dtype=np.float32) / np.float32(D))).astype(np.float32)
    ang = np.arange(256, dtype=np.float32)[:, None] * inv[None, :]
    ang = np.concatenate([ang] + [ang[:, :4]] * 4, 1)
    cos = np.repeat(np.cos(ang), 2, 1)
    sin = np.stack([-np.sin(ang), np.sin(ang)], -1).reshape(256, 160)
    return [np.ascontiguousarray(x.astype(np.float32).reshape(2, P, 160).transpose(1, 0, 2)) for x in (cos, sin)]


def layout(v):
    def c(x):
        return np.ascontiguousarray(x)

    def swapped(w):
        return w.reshape(D, -1, 2)[:, :, ::-1].reshape(w.shape)
    aq, ak, av = (np.asarray(v["L1_attn_W" + n]) for n in "qkv")
    cos, sin = rotation()
    fc, pj = v["L0_ffn_expert_fc"], v["L0_ffn_expert_proj"]
    return {
        "x": c(np.asarray(v["L0_attn_x"]).reshape(TOKENS, D)),
        "fc": c(np.asarray(fc).transpose(1, 0, 2).reshape(D, -1)),
        "pj": c(np.asarray(pj).reshape(8, D, 4, P).transpose(3, 0, 2, 1).reshape(P, -1)),
        "rw0": c(np.asarray(v["L0_ffn_router_w"]).T),
        "wg": c(np.asarray(v["L1_ffn_gate_w"]).transpose(2, 0, 1).reshape(D, -1)),
        "wu": c(np.asarray(v["L1_ffn_up_w"]).transpose(2, 0, 1).reshape(D, -1)),
        "wd": c(np.asarray(v["L1_ffn_down_w"]).transpose(2, 0, 1).reshape(P, -1)),
        "sg": c(np.asarray(v["L1_ffn_sgate_w"]).T),
        "su": c(np.asarray(v["L1_ffn_sup_w"]).T),
        "sd": c(np.asarray(v["L1_ffn_sdown_w"]).reshape(D, 4, P).transpose(2, 1, 0).reshape(P, -1)),
        "rw1": c(np.asarray(v["L1_ffn_router_w"]).T),
        "bias": c(np.broadcast_to(np.asarray(v["L1_ffn_router_bias"]), (P, 32))),
        "wqT": c(np.asarray(v["L0_attn_wq"]).reshape(D, HEADS, P).transpose(2, 1, 0).reshape(P, -1)),
        "woh": c(np.asarray(v["L0_attn_wo"]).reshape(HEADS, P, D).transpose(1, 0, 2).reshape(P, -1)),
        "wkdT": c(np.asarray(v["L0_attn_wk_down"]).reshape(D, KV, LAT).transpose(2, 1, 0).reshape(LAT, -1)),
        "wvdT": c(np.asarray(v["L0_attn_wv_down"]).reshape(D, KV, LAT).transpose(2, 1, 0).reshape(LAT, -1)),
        "aqkv": c(np.concatenate([aq, ak, swapped(aq), swapped(ak), av], 1)),
        "awo": c(np.asarray(v["L1_attn_Wo"])),
        "acos": cos,
        "asin": sin,
        "wku": c(np.asarray(v["L0_attn_wk_up"])),
        "wvu": c(np.asarray(v["L0_attn_wv_up"])),
    }


def kernel(**inputs):
    import concourse.bacc as bacc
    from concourse.bass_utils import run_bass_kernel_spmd

    nc = bacc.Bacc("TRN2", target_bir_lowering=False, num_devices=1)
    laid = layout(inputs)
    arrays = {f"in_{n}": laid[n] for n in INS}
    aps = {n: nc.dram_tensor(f"in_{n}", laid[n].shape, F32, kind="ExternalInput").ap() for n in INS}
    out = nc.dram_tensor("out", (TOKENS, D), F32, kind="ExternalOutput").ap()
    build(nc, aps, out)
    r = run_bass_kernel_spmd(nc, [arrays], core_ids=[0])
    return r.results[0]["out"].reshape(16, 256, 128)
```
